# Optimizing a Trainium2 kernel written in Bass

```python
import numpy as np
import jax
import jax.numpy as jnp

def _softmax(x, axis=-1):
    return jax.nn.softmax(x, axis=axis)

def _gelu(x):
    return jax.nn.gelu(x, approximate=True)

def _silu(x):
    return jax.nn.silu(x)

def _sigmoid(x):
    return jax.nn.sigmoid(x)

def _layernorm(x, axis=-1, eps=1e-05):
    m = jnp.mean(x, axis=axis, keepdims=True)
    v = jnp.var(x, axis=axis, keepdims=True)
    return (x - m) / jnp.sqrt(v + eps)

def _scatter_add(tgt, idx, src, axis=0):
    return tgt.at[idx].add(src)

def _segment_sum(src, seg, n):
    return jax.ops.segment_sum(src, seg, n)
kernel_name = 'mk_adj_resnorm_d2_adj_r2_d3a5c9'

def setup_inputs(seed: int=0):
    np.random.seed(seed)
    _w = jnp.asarray

    def _rec_inputs():
        import jax
        import jax.numpy as jnp
        _gk = jax.random.key(seed)
        x = -0.0002928 + 1 * jax.random.normal(jax.random.fold_in(_gk, 1), (2048, 256), jnp.float32)
        _a = jax.random.bernoulli(jax.random.fold_in(_gk, 2), 0.000976562, (2048, 2048))
        adj = _a
        return (x, adj)
    x, adj = _rec_inputs()

    def _L0_gnn_setup():
        import jax, jax.numpy as jnp
        import numpy as np
        N = 4096
        D = 256
        NEG = -1e+30
        key = jax.random.key(seed)
        ks = jax.random.split(key, 5)
        neuron_states = jax.random.normal(ks[0], (N, D), dtype=jnp.float32)
        adjacency = jax.random.bernoulli(ks[1], 0.05, (N, N))
        Wq = jax.random.normal(ks[2], (D, D), dtype=jnp.float32) / np.sqrt(D)
        Wk = jax.random.normal(ks[3], (D, D), dtype=jnp.float32) / np.sqrt(D)
        Wv = jax.random.normal(ks[4], (D, D), dtype=jnp.float32) / np.sqrt(D)
        return {'neuron_states': neuron_states, 'adjacency': adjacency, 'Wq': Wq, 'Wk': Wk, 'Wv': Wv}
    _L0_gnn_all = _L0_gnn_setup()
    _L0_gnn_in = {k: v for k, v in _L0_gnn_all.items() if k in ('Wq', 'Wk', 'Wv')}
    del _L0_gnn_all

    def _L1_gnn_setup():
        import jax, jax.numpy as jnp
        import numpy as np
        N = 4096
        D = 256
        NEG = -1e+30
        key = jax.random.key(seed)
        ks = jax.random.split(key, 5)
        neuron_states = jax.random.normal(ks[0], (N, D), dtype=jnp.float32)
        adjacency = jax.random.bernoulli(ks[1], 0.05, (N, N))
        Wq = jax.random.normal(ks[2], (D, D), dtype=jnp.float32) / np.sqrt(D)
        Wk = jax.random.normal(ks[3], (D, D), dtype=jnp.float32) / np.sqrt(D)
        Wv = jax.random.normal(ks[4], (D, D), dtype=jnp.float32) / np.sqrt(D)
        return {'neuron_states': neuron_states, 'adjacency': adjacency, 'Wq': Wq, 'Wk': Wk, 'Wv': Wv}
    _L1_gnn_all = _L1_gnn_setup()
    _L1_gnn_in = {k: v for k, v in _L1_gnn_all.items() if k in ('Wq', 'Wk', 'Wv')}
    del _L1_gnn_all
    return {'x': x, 'adj': adj, 'L0_gnn_Wq': _L0_gnn_in['Wq'], 'L0_gnn_Wk': _L0_gnn_in['Wk'], 'L0_gnn_Wv': _L0_gnn_in['Wv'], 'L1_gnn_Wq': _L1_gnn_in['Wq'], 'L1_gnn_Wk': _L1_gnn_in['Wk'], 'L1_gnn_Wv': _L1_gnn_in['Wv']}

def reference(x, adj, L0_gnn_Wq, L0_gnn_Wk, L0_gnn_Wv, L1_gnn_Wq, L1_gnn_Wk, L1_gnn_Wv):
    import jax
    import jax.numpy as jnp

    def _L0_gnn_ref(neuron_states, adjacency, Wq, Wk, Wv):
        import jax, jax.numpy as jnp
        import numpy as np
        N = 4096
        D = 256
        NEG = -1e+30
        q = neuron_states @ Wq.T
        k = neuron_states @ Wk.T
        v = neuron_states @ Wv.T
        mask = adjacency.T
        scores = jnp.where(mask, q @ k.T, NEG)
        attn = jax.nn.softmax(scores, axis=1)
        attn = jnp.where(mask, attn, 0.0)
        return attn @ v

    def _L1_gnn_ref(neuron_states, adjacency, Wq, Wk, Wv):
        import jax, jax.numpy as jnp
        import numpy as np
        N = 4096
        D = 256
        NEG = -1e+30
        q = neuron_states @ Wq.T
        k = neuron_states @ Wk.T
        v = neuron_states @ Wv.T
        mask = adjacency.T
        scores = jnp.where(mask, q @ k.T, NEG)
        attn = jax.nn.softmax(scores, axis=1)
        attn = jnp.where(mask, attn, 0.0)
        return attn @ v
    x = _layernorm(x + _L0_gnn_ref(x, adj, L0_gnn_Wq, L0_gnn_Wk, L0_gnn_Wv), axis=-1)
    x = _layernorm(x + _L1_gnn_ref(x, adj, L1_gnn_Wq, L1_gnn_Wk, L1_gnn_Wv), axis=-1)
    return x

_drawn_inputs = setup_inputs


def setup_inputs(seed=0):
    import zlib

    import numpy as np

    out = dict(_drawn_inputs(seed))
    spreads = {}
    factors = {}
    for name, (base, spread) in spreads.items():
        noise = np.random.default_rng([zlib.crc32(name.encode()), seed]).standard_normal(out[name].shape)
        drawn = base * np.exp(spread * noise) if base else spread * noise
        out[name] = jnp.asarray(drawn.astype(out[name].dtype))
    for name, factor in factors.items():
        out[name] = (out[name] * factor).astype(out[name].dtype)
    return out
```

```python
import concourse.bass as bass
from concourse import mybir
from contextlib import ExitStack

F32 = mybir.dt.float32
BF16 = mybir.dt.bfloat16
FP8 = mybir.dt.float8e4
U8 = mybir.dt.uint8
U32 = mybir.dt.uint32
ALU = mybir.AluOpType
ACT = mybir.ActivationFunctionType
AX = mybir.AxisListType.X

P = 128
N = 2048
D = 256
T = N // P
H = D // P
LAYERS = 2
EPS = 1e-5
TRUE_AS_FP8 = 2.0 ** -9
NO_EDGE = -(2.0 ** 100)


def build(nc, x, adj, wq, wk, wv, out):
    ctx = ExitStack()
    with ctx:
        def sb(name, shape, dt):
            return ctx.enter_context(nc.sbuf_tensor(name, shape, dt))

        def pb(name, shape, dt):
            return ctx.enter_context(nc.psum_tensor(name, shape, dt))

        def sem(name):
            return ctx.enter_context(nc.semaphore(name))

        X = [sb(f"X{n}", [P, T, D], F32) for n in range(LAYERS + 1)]
        A = sb("A", [P, T, N // 4], U32)
        W = sb("W", [P, LAYERS, 3, H, D], F32)
        M = sb("M", [P, LAYERS, H, D], F32)
        WvT = sb("WvT", [P, LAYERS, H, D], F32)
        ident = sb("ident", [P, P], F32)
        no_edge_ident = sb("no_edge_ident", [P, P], BF16)
        stage = sb("stage", [P, D], F32)
        xT = sb("xT", [P, H, N], F32)
        qT = sb("qT", [P, H, P], F32)
        not_adj = sb("not_adj", [P, T, P // 4], U32)
        top = sb("top", [P, 1], F32)
        neg_top = sb("neg_top", [P, 1], F32)
        has_edge = sb("has_edge", [P, 1], F32)
        total = sb("total", [P, 1], F32)
        inv = sb("inv", [P, 1], F32)
        inv2 = sb("inv2", [P, 1], F32)
        prob = sb("prob", [P, N], F32)
        probT = sb("probT", [P, T, P], F32)
        yT = sb("yT", [P, H, P], F32)
        stats = sb("stats", [P, 6], F32)
        hrow = sb("hrow", [P, D], F32)
        started = sb("started", [P, 4], F32)
        st = sb("st", [P, T, 6], F32)
        mean2, gap, m2, mean, gap2, m2e, var_out = (sb(n, [P, T], F32) for n in "mean2 gap m2 mean gap2 m2e var_out".split())
        var_eps = sb("var_eps", [P, T], F32)
        std = sb("std", [P, T], F32)
        rstd = sb("rstd", [P, T], F32)

        S = pb("S", [P, N], F32)
        psT = [pb(f"psT{n}", [P, 4, P], F32) for n in range(2)]
        psA = pb("psA", [P, H, D], F32)
        psB = pb("psB", [P, H, D], F32)

        names = ("x_in w_in a_in ident_set consts m_ps m_sb wv_ps wv_sb staged xt_ps xt_sb q_ps q_sb slab scored "
                 "topped neg_topped exped t_ps t_act t_dve y_ps y_sb o_ps res stat moments summed inved inv2ed "
                 "var_ready std_ready rstd_ready normed stored ln kept").split()
        s = {n: sem(n) for n in names}
        block = ctx.enter_context(nc.Block())

        @block.sync
        def _(eng):
            for L in range(LAYERS):
                for n, w in enumerate((wq[L], wk[L], wv[L])):
                    eng.dma_start(W[:, L, n, :, :], w.rearrange("(h p) d -> p h d", p=P)).then_inc(s["w_in"], 16)
            eng.dma_start(X[0][:, :, :], x.rearrange("(t p) d -> p t d", p=P)).then_inc(s["x_in"], 16)
            for c in range(4):
                eng.dma_start(A[:, 4 * c:4 * c + 4, :],
                              adj[512 * c:512 * c + 512, :].rearrange("(t p) n -> p t n", p=P)).then_inc(s["a_in"], 16)
            eng.wait_ge(s["normed"], LAYERS * T)
            eng.dma_start(out.rearrange("(t p) d -> p t d", p=P), X[LAYERS][:, :, :]).then_inc(s["stored"], 16)
            eng.wait_ge(s["stored"], 16)

        @block.gpsimd
        def _(eng):
            eng.memset(ident[:, :], 0.0).then_inc(s["ident_set"], 1)
            eng.memset(no_edge_ident[:, :], 0.0).then_inc(s["ident_set"], 1)
            eng.wait_ge(s["ident_set"], 2)
            eng.affine_select(out=ident[:, :], in_=ident[:, :], compare_op=ALU.not_equal, fill=1.0,
                              base=0, pattern=[[-1, P]], channel_multiplier=1).then_inc(s["consts"], 1)
            eng.affine_select(out=no_edge_ident[:, :], in_=no_edge_ident[:, :], compare_op=ALU.not_equal,
                              fill=NO_EDGE / TRUE_AS_FP8, base=0, pattern=[[-1, P]],
                              channel_multiplier=1).then_inc(s["consts"], 1)
            for L in range(LAYERS):
                if L == 0:
                    eng.wait_ge(s["x_in"], 16)
                else:
                    eng.wait_ge(s["normed"], L * T)
                with eng.Fori(0, T) as t:
                    if True:
                        eng.wait_ge(s["xt_ps"], t + L * T + 1)
                    eng.tensor_copy(stage[:, :], X[L][:, bass.ds(t, 1), :].rearrange("p a d -> p (a d)")).then_inc(s["staged"], 1)
                with eng.Fori(0, T) as t:
                    eng.wait_ge(s["res"], t + (L * T + 1) + 1)
                    eng.tensor_copy(X[L + 1][:, bass.ds(t, 1), :].rearrange("p a d -> p (a d)"), hrow[:, :]).then_inc(s["kept"], 1)

        @block.scalar
        def _(act):
            for L in range(LAYERS):
                act.wait_ge(s["m_ps"], L + 1)
                act.activation(M[:, L, :, :], psA[:, :, :], ACT.Copy).then_inc(s["m_sb"], 1)
                act.wait_ge(s["wv_ps"], L + 1)
                act.activation(WvT[:, L, :, :], psB[:, :, :], ACT.Copy).then_inc(s["wv_sb"], 1)
            for L in range(LAYERS):
                with act.Fori(0, T) as t:
                    act.wait_ge(s["xt_ps"], t + (L * T + 1) + 1)
                    act.activation(xT[:, :, bass.ds(t * P, P)], psA[:, 0, :].rearrange("p (h n) -> p h n", h=H),
                                   ACT.Copy).then_inc(s["xt_sb"], 1)
                with act.Fori(0, T) as t:
                    act.wait_ge(s["q_ps"], t + (L * T + 1))
                    act.activation(qT[:, :, :], psA[:, 0, :].rearrange("p (h n) -> p h n", h=H),
                                   ACT.Copy).then_inc(s["q_sb"], 1)
                    act.wait_ge(s["neg_topped"], t + (L * T + 1))
                    act.activation(prob[:, :], S[:, :], ACT.Exp, bias=neg_top[:, :],
                                   accum_out=total[:, :]).then_inc(s["exped"], 1)
                    for g in (1, 3):
                        act.wait_ge(s["t_ps"], t * 4 + (L * T * 4 + g + 1))
                        act.activation(probT[:, 4 * g:4 * g + 4, :], psT[1][:, :, :], ACT.Copy).then_inc(s["t_act"], 1)
                    act.wait_ge(s["y_ps"], t + (L * T + 1))
                    act.activation(yT[:, :, :], psB[:, 0, :].rearrange("p (h n) -> p h n", h=H),
                                   ACT.Copy).then_inc(s["y_sb"], 1)
                act.wait_ge(s["var_ready"], L + 1)
                act.activation(std[:, :], var_out[:, :], ACT.Sqrt).then_inc(s["std_ready"], 1)

        @block.vector
        def _(dve):
            for c, n in enumerate(("xt_ps", "xt_sb", "res", "kept")):
                dve.memset(started[:, c:c + 1], 0.0).then_inc(s[n], 1)
            dve.wait_ge(s["a_in"], 64)
            for L in range(LAYERS):
                with dve.Fori(0, T) as t:
                    dve.tensor_scalar(not_adj[:, :, :], A[:, :, bass.ds(t * (P // 4), P // 4)], 0x01010101, None,
                                      ALU.bitwise_xor).then_inc(s["slab"], 1)
                    dve.wait_ge(s["scored"], t + (L * T + 1))
                    dve.reduce_max(top[:, :], S[:, :], axis=AX).then_inc(s["topped"], 1)
                    dve.wait_ge(s["topped"], t + (L * T + 1))
                    dve.tensor_scalar(neg_top[:, :], top[:, :], -1.0, None, ALU.mult).then_inc(s["neg_topped"], 1)
                    dve.tensor_scalar(has_edge[:, :], top[:, :], NO_EDGE / 2, None, ALU.is_gt).then_inc(s["moments"], 1)
                    dve.wait_ge(s["exped"], t + (L * T + 1))
                    dve.reciprocal(inv[:, :], total[:, :]).then_inc(s["inved"], 1)
                    dve.wait_ge(s["inved"], t + (L * T + 1))
                    dve.tensor_tensor(inv2[:, :], inv[:, :], has_edge[:, :], ALU.mult).then_inc(s["inv2ed"], 1)
                    for g in (0, 2):
                        dve.wait_ge(s["t_ps"], t * 4 + (L * T * 4 + g + 1))
                        dve.tensor_copy(probT[:, 4 * g:4 * g + 4, :], psT[0][:, :, :]).then_inc(s["t_dve"], 1)
                    dve.wait_ge(s["o_ps"], t + (L * T + 1))
                    if True:
                        dve.wait_ge(s["kept"], t + L * T + 1)
                    dve.scalar_tensor_tensor(out=hrow[:, :], in0=psA[:, 1, :], scalar=inv2[:, :],
                                             in1=X[L][:, bass.ds(t, 1), :].rearrange("p a d -> p (a d)"),
                                             op0=ALU.mult, op1=ALU.add).then_inc(s["res"], 1)
                    dve.wait_ge(s["res"], t + (L * T + 1) + 1)
                    dve.bn_stats(stats[:, :], hrow[:, :]).then_inc(s["stat"], 1)
                    dve.wait_ge(s["stat"], t + (L * T + 1))
                    dve.tensor_copy(st[:, bass.ds(t, 1), :].rearrange("p a d -> p (a d)"), stats[:, :]).then_inc(s["summed"], 1)
                dve.wait_ge(s["summed"], T * (L + 1))
                dve.tensor_tensor(mean2[:, :], st[:, :, 1], st[:, :, 4], ALU.add).then_inc(s["ln"], 1)
                dve.tensor_tensor(gap[:, :], st[:, :, 1], st[:, :, 4], ALU.subtract).then_inc(s["ln"], 1)
                dve.tensor_tensor(m2[:, :], st[:, :, 2], st[:, :, 5], ALU.add).then_inc(s["ln"], 1)
                dve.wait_ge(s["ln"], 7 * L + 3)
                dve.tensor_scalar(mean[:, :], mean2[:, :], 0.5, None, ALU.mult).then_inc(s["ln"], 1)
                dve.scalar_tensor_tensor(out=gap2[:, :], in0=gap[:, :], scalar=0.25, in1=gap[:, :],
                                         op0=ALU.mult, op1=ALU.mult).then_inc(s["ln"], 1)
                dve.tensor_scalar(m2e[:, :], m2[:, :], 1.0 / D, EPS, ALU.mult, ALU.add).then_inc(s["ln"], 1)
                dve.wait_ge(s["ln"], 7 * L + 6)
                dve.tensor_tensor(var_eps[:, :], m2e[:, :], gap2[:, :], ALU.add).then_inc(s["ln"], 1)
                dve.wait_ge(s["ln"], 7 * L + 7)
                dve.tensor_copy(var_out[:, :], var_eps[:, :]).then_inc(s["var_ready"], 1)
                dve.wait_ge(s["std_ready"], L + 1)
                dve.reciprocal(rstd[:, :], std[:, :]).then_inc(s["rstd_ready"], 1)
                dve.wait_ge(s["rstd_ready"], L + 1)
                dve.wait_ge(s["kept"], T * (L + 1) + 1)
                with dve.Fori(0, T) as t:
                    xn = X[L + 1][:, bass.ds(t, 1), :].rearrange("p a d -> p (a d)")
                    dve.tensor_scalar(xn, xn, mean[:, bass.ds(t, 1)], rstd[:, bass.ds(t, 1)],
                                      ALU.subtract, ALU.mult).then_inc(s["normed"], 1)

        @block.tensor
        def _(pe):
            pe.wait_ge(s["w_in"], 16 * 3 * LAYERS)
            pe.wait_ge(s["consts"], 2)
            for L in range(LAYERS):
                if L > 0:
                    pe.wait_ge(s["m_sb"], L)
                for h in range(H):
                    for e in range(H):
                        last = nc.tensor.matmul(psA[:, h, :], W[:, L, 0, e, h * P:h * P + P], W[:, L, 1, e, :],
                                                start=(e == 0), stop=(e == H - 1))
                last.then_inc(s["m_ps"], 1)
                if L > 0:
                    pe.wait_ge(s["wv_sb"], L)
                for h in range(H):
                    for e in range(H):
                        last = nc.tensor.transpose(psB[:, h, e * P:e * P + P], W[:, L, 2, e, h * P:h * P + P],
                                                   ident[:, :])
                last.then_inc(s["wv_ps"], 1)
            for L in range(LAYERS):
                with pe.Fori(0, T) as t:
                    pe.wait_ge(s["staged"], t + (L * T + 1))
                    if L == 0:
                        pe.wait_ge(s["m_sb"], LAYERS)
                    pe.wait_ge(s["xt_sb"], t + L * T + 1)
                    for h in range(H):
                        last = nc.tensor.transpose(psA[:, 0, h * P:h * P + P], stage[:, h * P:h * P + P], ident[:, :])
                    last.then_inc(s["xt_ps"], 1)
                pe.wait_ge(s["xt_sb"], T * (L + 1) + 1)
                with pe.Fori(0, T) as t:
                    pe.wait_ge(s["res"], t + L * T + 1)
                    pe.wait_ge(s["slab"], t + (L * T + 1))
                    for h in range(H):
                        for e in range(H):
                            last = nc.tensor.matmul(psA[:, 0, h * P:h * P + P], M[:, L, e, h * P:h * P + P],
                                                    xT[:, e, bass.ds(t * P, P)], start=(e == 0), stop=(e == H - 1))
                    last.then_inc(s["q_ps"], 1)
                    for j in range(T):
                        nc.tensor.matmul(S[:, j * P:j * P + P], not_adj[:, j, :].bitcast(FP8), no_edge_ident[:, :],
                                         start=(j % 4 == 0), stop=False, skip_group_check=True)
                    pe.wait_ge(s["q_sb"], t + (L * T + 1))
                    for h in range(H):
                        for c in range(4):
                            last = nc.tensor.matmul(S[:, c * 512:c * 512 + 512], qT[:, h, :],
                                                    xT[:, h, c * 512:c * 512 + 512], start=False, stop=(h == H - 1),
                                                    skip_group_check=True)
                    last.then_inc(s["scored"], 1)
                    pe.wait_ge(s["exped"], t + (L * T + 1))
                    for g in range(4):
                        if g == 2:
                            pe.wait_ge(s["t_dve"], t * 2 + (L * T * 2 + 1))
                        if g == 3:
                            pe.wait_ge(s["t_act"], t * 2 + (L * T * 2 + 1))
                        for k in range(4):
                            j = 4 * g + k
                            last = nc.tensor.transpose(psT[g % 2][:, k, :], prob[:, j * P:j * P + P], ident[:, :])
                        last.then_inc(s["t_ps"], 1)
                    pe.wait_ge(s["t_dve"], t * 2 + (L * T * 2 + 2))
                    pe.wait_ge(s["t_act"], t * 2 + (L * T * 2 + 2))
                    for h in range(H):
                        for j in range(T):
                            last = nc.tensor.matmul(psB[:, 0, h * P:h * P + P], X[L][:, j, h * P:h * P + P],
                                                    probT[:, j, :], start=(j == 0), stop=(j == T - 1))
                    last.then_inc(s["y_ps"], 1)
                    pe.wait_ge(s["y_sb"], t + (L * T + 1))
                    for h in range(H):
                        last = nc.tensor.matmul(psA[:, 1, :], yT[:, h, :], WvT[:, L, h, :],
                                                start=(h == 0), stop=(h == H - 1))
                    last.then_inc(s["o_ps"], 1)


def kernel(**inputs):
    import numpy as np
    import concourse.bacc as bacc
    from concourse.bass_utils import run_bass_kernel_spmd as run

    nc = bacc.Bacc("TRN2", target_bir_lowering=False, num_devices=1)
    arrays, ap = {}, {}
    for name, value in inputs.items():
        a = np.ascontiguousarray(value)
        if a.dtype == np.bool_:
            a = a.view(np.uint32)
        arrays[f"in_{name}"] = a
        ap[name] = nc.dram_tensor(f"in_{name}", a.shape, mybir.dt.from_np(a.dtype), kind="ExternalInput").ap()
    out = nc.dram_tensor("out", (N, D), F32, kind="ExternalOutput").ap()
    w = {k: [ap[f"L{L}_gnn_W{k}"] for L in range(LAYERS)] for k in "qkv"}
    build(nc, ap["x"], ap["adj"], w["q"], w["k"], w["v"], out)
    return run(nc, [arrays], core_ids=[0]).results[0]["out"]
```

```python
import concourse.bass as bass
from concourse import mybir
from contextlib import ExitStack

F32 = mybir.dt.float32
F16 = mybir.dt.float16
BF16 = mybir.dt.bfloat16
FP8 = mybir.dt.float8e4
U32 = mybir.dt.uint32
I32 = mybir.dt.int32
ALU = mybir.AluOpType
ACT = mybir.ActivationFunctionType
AX = mybir.AxisListType.X

P = 128
N = 2048
D = 256
T = N // P
H = D // P
LAYERS = 2
EPS = 1e-5
BANK = 512
TRUE_AS_FP8 = 2.0 ** -9
NO_EDGE = -(2.0 ** 100)

G = 16
NW = N // G
WT = P // G
K = 16
U = 3
E = U * P
RING = 4
LR = K + 2
LP = 64


def edges_and_dense(nc, x, adj, wq, wk, wv, out):
    ctx = ExitStack()
    with ctx:
        def sb(name, shape, dt=F32):
            return ctx.enter_context(nc.sbuf_tensor(name, shape, dt))

        def sem(name):
            return ctx.enter_context(nc.semaphore(name))

        x1_dram = nc.dram_tensor("x1_rows", (N, D), F32, kind="Internal").ap()

        X0 = sb("X0", [P, T, D])
        X1 = sb("X1", [P, T, D])
        X = [X0, X1, X0]
        adj_words = sb("adj_words", [P, T, N // 4], U32)
        W = sb("W", [P, LAYERS, 3, H, D])
        M = sb("M", [P, LAYERS, H, D])
        WvT = sb("WvT", [P, LAYERS, H, D])
        ident = sb("ident", [P, P])
        bn = sb("bn", [P, T, 6])
        mean2, gap, m2, mean, gap2, m2e, var_eps, std, rstd = (
            sb(n, [P, T]) for n in "mean2 gap m2 mean gap2 m2e var_eps std rstd".split())
        stage = sb("stage", [P, RING, D])
        started = sb("started", [P, 8])

        ones = sb("ones", [P, P])
        before = sb("before", [P, P])
        iota = sb("iota", [P, E], F16)
        iota_w = sb("iota_w", [P, NW])
        iota_k = sb("iota_k", [P, K])
        iota_e = sb("iota_e", [P, U])
        row = sb("row", [P, 1], I32)
        row_lo = sb("row_lo", [P, 1], I32)
        row_exp = sb("row_exp", [P, 1], I32)
        row_pow = sb("row_pow", [P, 1], I32)
        row_f = sb("row_f", [P, 1])
        group = sb("group", [P, WT])
        pack = sb("pack", [P, WT], BF16)
        key = X1[:, 0:T * NW // D, :].rearrange("p a (b w) -> p (a b) w", w=NW)
        top_words = sb("top_words", [P, T, K])
        top_u = sb("top_u", [P, T, K], U32)
        word_u, bits_u, first_e, second_e = (sb(n, [P, T, K], U32) for n in "word_u bits_u first_e second_e".split())
        bits_f, first_p, rest, second_p, rest2, base, code1, code2 = (
            sb(n, [P, T, K]) for n in "bits_f first_p rest second_p rest2 base code1 code2".split())
        codes = sb("codes", [P, T, 2 * K])
        nbr = sb("nbr", [P, T, K])
        deg = sb("deg", [P, T])
        off = sb("off", [P, T])
        end = sb("end", [P, T])
        count = sb("count", [P, 1])
        over = sb("over", [P, 4])
        over1 = sb("over1", [P, 1])
        over2 = sb("over2", [P, 1])
        over_i = sb("over_i", [P, 1], I32)
        per_query = sb("per_query", [P, T, LR], F16)
        step = sb("step", [P, E], F16)
        own = sb("own", [P, T, E], F16)
        own_t = sb("own_t", [P, T, U, P], F16)
        L = sb("L", [P, T, U, LR])
        k_of = sb("k_of", [P, T, U])
        k_hot = sb("k_hot", [P, T, U, K])
        picked = sb("picked", [P, T, U, K])
        code_e = sb("code_e", [P, T, U])
        key_row = sb("key_row", [P, T, U], U32)
        no_slot = sb("no_slot", [P, T, K])

        Q = sb("Q", [P, T, D])
        xt = sb("xt", [P, RING, H, P])
        own_f = sb("own_f", [P, RING, E])
        own_tf = sb("own_tf", [P, RING, U, P])
        xg = sb("xg", [P, RING, U, D])
        prod = sb("prod", [P, U, D])
        score = sb("score", [P, RING, U])
        score_k = sb("score_k", [P, RING, U, K])
        masked = sb("masked", [P, 2, K])
        neg_top = sb("neg_top", [P, 2, 1])
        exps = sb("exps", [P, 2, K])
        total = sb("total", [P, RING, 1])
        inv = sb("inv", [P, RING, 1])
        shifted = sb("shifted", [P, RING, U])
        prob = sb("prob", [P, RING, U])
        weight = sb("weight", [P, RING, U, P])
        y_sb = sb("y_sb", [P, H, P])

        all_xT = Q[:, :, :].rearrange("p t d -> p (t d)").rearrange("p (h n) -> p h n", h=H)
        all_prob = own[:, :, :].rearrange("p t e -> p (t e)").bitcast(F32)[:, 0:N]
        all_probT = own_t[:, :, :, :].rearrange("p t u q -> p (t u q)").bitcast(F32)[:, 0:N].rearrange(
            "p (t q) -> p t q", t=T)
        not_adj = sb("not_adj", [P, T, P // 4], U32)
        no_edge_ident = sb("no_edge_ident", [P, P], BF16)
        one_row = sb("one_row", [P, D])
        one_qT = sb("one_qT", [P, H, P])
        new_row = sb("new_row", [P, D])
        bn_row = sb("bn_row", [P, 6])
        row_top, row_neg_top, row_has, row_total, row_inv, row_scale = (
            sb(n, [P, 1]) for n in "row_top row_neg_top row_has row_total row_inv row_scale".split())

        PS = ctx.enter_context(nc.psum_tensor("PS", [P, 8, BANK], F32))

        names = """w_in x_in memsets consts dc packed c keys tops nbrs off_ps listed own_ready l_ps l_sb listed_e
            own_t_ready over_ready flag_ps flag m_ps m_sb staged xt_ps xt_sb q_ps q_sb
            own_f_ready own_tf_ready qe_ready s_done sk_in sk_ready maxed mask_done me_ready ds_ready
            totalled p_ready a_ready y_ready y_sb_ready o_ready inved res bn_done ln var_ready std_ready
            rstd_ready normed x1_stored stored""".split()
        s = {n: sem(n) for n in names}
        names = """x_again no_edge_set no_edge staged xt_ps xt_sb q_ps q_sb slab scored topped neg_topped has exped
            t_ps t_act t_dve y_ps y_sb o_ps res stat moved inved scaled ln var_ready std_ready rstd_ready kept
            normed stored""".split()
        sa = {n: sem("all_" + n) for n in names}
        a_in = [sem(f"a_in{c}") for c in range(4)]
        gathered = [sem(f"gathered{c}") for c in range(RING)]
        block = ctx.enter_context(nc.Block())

        def steps(eng, last_lag, body):
            for v in range(RING):
                body(v, 0, v)
            with eng.Fori(1, T // RING) as g:
                for u in range(RING):
                    body(g * RING + u, g, u)
            for u in range(last_lag):
                body(T + u, T // RING, u)

        def too_many(eng):
            eng.wait_ge(s["flag"], 1)
            return eng.If(eng.value_load(over_i[0:1, 0:1], min_val=0, max_val=P))

        def at(v, g, u, lag):
            if isinstance(v, int):
                if not 0 <= v - lag < T:
                    return None
                return v - lag, (v - lag) % RING, (v - lag) // RING
            return g * RING + (u - lag), (u - lag) % RING, g + (u - lag) // RING

        def need(eng, name, value):
            if not isinstance(value, int) or value > 0:
                eng.wait_ge(s[name] if isinstance(name, str) else name, value)

        def tile(ap, t):
            return ap[:, bass.ds(t, 1), :].rearrange("p a d -> p (a d)")

        @block.sync
        def _(sp):
            for c in range(4):
                sp.dma_start(adj_words[:, 4 * c:4 * c + 4, :],
                             adj[512 * c:512 * c + 512, :].rearrange("(t p) n -> p t n", p=P)).then_inc(a_in[c], 16)
            for layer, rows, name in ((0, x1_dram, "x1_stored"), (1, out, "stored")):
                for c in range(4):
                    sp.wait_ge(s["normed"], T * layer + 4 * (c + 1))
                    sp.dma_start(rows[512 * c:512 * c + 512, :].rearrange("(t p) d -> p t d", p=P),
                                 X[layer + 1][:, 4 * c:4 * c + 4, :]).then_inc(s[name], 16)
            sp.wait_ge(s["stored"], 64)

            with too_many(sp):
                sp.dma_start(X0[:, :, :], x.rearrange("(t p) d -> p t d", p=P)).then_inc(sa["x_again"], 16)
                sp.wait_ge(sa["normed"], LAYERS * T)
                sp.dma_start(out.rearrange("(t p) d -> p t d", p=P), X[LAYERS][:, :, :]).then_inc(sa["stored"], 16)
                sp.wait_ge(sa["stored"], 16)

        @block.gpsimd
        def _(pool):
            pool.memset(ident[:, :], 0.0).then_inc(s["memsets"], 1)
            pool.memset(group[:, :], 1.0).then_inc(s["memsets"], 1)
            pool.memset(before[:, :], 1.0).then_inc(s["memsets"], 1)
            pool.iota(row[:, :], pattern=[[0, 1]], base=0, channel_multiplier=1).then_inc(s["consts"], 1)
            pool.wait_ge(s["memsets"], 3)
            pool.affine_select(out=group[:, :], in_=group[:, :], compare_op=ALU.is_ge, fill=0.0, base=0,
                               pattern=[[-G, WT]], channel_multiplier=1).then_inc(s["memsets"], 1)
            pool.wait_ge(s["memsets"], 4)
            pool.affine_select(out=group[:, :], in_=group[:, :], compare_op=ALU.is_ge, fill=0.0, base=G - 1,
                               pattern=[[G, WT]], channel_multiplier=-1).then_inc(s["consts"], 1)
            pool.affine_select(out=ident[:, :], in_=ident[:, :], compare_op=ALU.not_equal, fill=1.0, base=0,
                               pattern=[[-1, P]], channel_multiplier=1).then_inc(s["consts"], 1)
            pool.affine_select(out=before[:, :], in_=before[:, :], compare_op=ALU.is_ge, fill=0.0, base=-1,
                               pattern=[[1, P]], channel_multiplier=-1).then_inc(s["consts"], 1)
            pool.memset(ones[:, :], 1.0).then_inc(s["consts"], 1)
            pool.iota(iota[:, :], pattern=[[1, E]], base=0, channel_multiplier=0,
                      allow_small_or_imprecise_dtypes=True).then_inc(s["consts"], 1)
            pool.iota(iota_w[:, :], pattern=[[1, NW]], base=0, channel_multiplier=0,
                      allow_small_or_imprecise_dtypes=True).then_inc(s["consts"], 1)
            pool.iota(iota_k[:, :], pattern=[[1, K]], base=0, channel_multiplier=0,
                      allow_small_or_imprecise_dtypes=True).then_inc(s["consts"], 1)
            pool.iota(iota_e[:, :], pattern=[[P, U]], base=0, channel_multiplier=1,
                      allow_small_or_imprecise_dtypes=True).then_inc(s["consts"], 1)
            pool.iota(row_f[:, :], pattern=[[0, 1]], base=1, channel_multiplier=1,
                      allow_small_or_imprecise_dtypes=True).then_inc(s["consts"], 1)

            pool.wait_ge(s["x_in"], 16)
            for layer in range(LAYERS):
                def copy_rows(v, g, u):
                    t, slot, _ = at(v, g, u, 0)
                    if layer > 0:
                        pool.wait_ge(s["normed"], t + ((layer - 1) * T + 1))
                    need(pool, "xt_ps", t + (layer * T - 3))
                    pool.tensor_copy(stage[:, slot, :], tile(X[layer], t)).then_inc(s["staged"], 1)
                steps(pool, 0, copy_rows)

                rows = x if layer == 0 else x1_dram
                if layer == 0:
                    pool.wait_ge(s["listed_e"], 1)
                else:
                    pool.wait_ge(s["x1_stored"], 64)
                for t in range(T):
                    need(pool, "y_ready", t + layer * T - 3)
                    for n in range(U):
                        pool.indirect_dma_start(xg[:, t % RING, n, :], None, rows,
                                                bass.IndirectOffsetOnAxis(ap=key_row[:, t, n:n + 1], axis=0),
                                                bounds_check=N - 1, oob_is_err=False).then_inc(gathered[t % RING], 16)

            with too_many(pool):
                pool.memset(no_edge_ident[:, :], 0.0).then_inc(sa["no_edge_set"], 1)
                pool.wait_ge(sa["no_edge_set"], 1)
                pool.affine_select(out=no_edge_ident[:, :], in_=no_edge_ident[:, :], compare_op=ALU.not_equal,
                                   fill=NO_EDGE / TRUE_AS_FP8, base=0, pattern=[[-1, P]],
                                   channel_multiplier=1).then_inc(sa["no_edge"], 1)
                for layer in range(LAYERS):
                    if layer == 0:
                        pool.wait_ge(sa["x_again"], 16)
                    else:
                        pool.wait_ge(sa["normed"], layer * T)
                    with pool.Fori(0, T) as t:
                        pool.wait_ge(sa["xt_ps"], t + (layer * T + 1))
                        pool.tensor_copy(one_row[:, :], tile(X[layer], t)).then_inc(sa["staged"], 1)
                    with pool.Fori(0, T) as t:
                        pool.wait_ge(sa["res"], t + (layer * T + 2))
                        pool.tensor_copy(tile(X[layer + 1], t), new_row[:, :]).then_inc(sa["kept"], 1)

        @block.scalar
        def _(act):
            for n in range(LAYERS):
                for i, w in enumerate((wq[n], wk[n], wv[n])):
                    act.dma_start(W[:, n, i, :, :], w.rearrange("(h p) d -> p h d", p=P)).then_inc(s["w_in"], 16)
            act.dma_start(X0[:, :, :], x.rearrange("(t p) d -> p t d", p=P)).then_inc(s["x_in"], 16)
            for n in range(LAYERS):
                act.wait_ge(s["m_ps"], 2 * n + 1)
                act.activation(M[:, n, :, :], PS[:, 6, :].rearrange("p (h d) -> p h d", h=H), ACT.Copy).then_inc(s["m_sb"], 1)
                act.wait_ge(s["m_ps"], 2 * n + 2)
                act.activation(WvT[:, n, :, :], PS[:, 7, :].rearrange("p (h d) -> p h d", h=H), ACT.Copy).then_inc(s["m_sb"], 1)

            for layer in range(LAYERS):
                def project(v, g, u):
                    if (now := at(v, g, u, 0)) is not None:
                        t, slot, _ = now
                        act.wait_ge(s["xt_ps"], t + (layer * T + 1))
                        act.activation(xt[:, slot, :, :], PS[:, 4 + slot % 2, 0:D].rearrange("p (h n) -> p h n", h=H),
                                       ACT.Copy).then_inc(s["xt_sb"], 1)
                    if (now := at(v, g, u, 1)) is not None:
                        t, slot, _ = now
                        act.wait_ge(s["q_ps"], t + (layer * T + 1))
                        act.activation(tile(Q, t), PS[:, 6 + slot % 2, 0:D], ACT.Copy).then_inc(s["q_sb"], 1)
                steps(act, 1, project)

                def over_edges(v, g, u):
                    if (now := at(v, g, u, 0)) is not None:
                        t, slot, _ = now
                        if layer == 0:
                            act.wait_ge(s["own_ready"], t + 1)
                        need(act, "me_ready", t + (layer * T - 3))
                        act.activation(own_f[:, slot, :], tile(own, t), ACT.Copy).then_inc(s["own_f_ready"], 1)
                        if layer == 0:
                            act.wait_ge(s["own_t_ready"], t + 1)
                        need(act, "a_ready", t * U + (layer * T - 3) * U)
                        act.activation(own_tf[:, slot, :, :],
                                       own_t[:, bass.ds(t, 1), :, :].rearrange("p a u n -> p (a u) n"),
                                       ACT.Copy).then_inc(s["own_tf_ready"], 1)
                    if (now := at(v, g, u, 3)) is not None:
                        t, slot, _ = now
                        act.wait_ge(s["y_ready"], t + (layer * T + 1))
                        act.activation(y_sb[:, :, :], PS[:, 6, 0:D].rearrange("p (h n) -> p h n", h=H),
                                       ACT.Copy).then_inc(s["y_sb_ready"], 1)
                    if (now := at(v, g, u, 2)) is not None:
                        t, slot, _ = now
                        act.wait_ge(s["maxed"], t + (layer * T + 1))
                        act.activation(exps[:, slot % 2, :], masked[:, slot % 2, :], ACT.Exp,
                                       bias=neg_top[:, slot % 2, :], scale=-1.0,
                                       accum_out=total[:, slot, :]).then_inc(s["totalled"], 1)
                        act.wait_ge(s["ds_ready"], t + (layer * T + 1))
                        act.activation(prob[:, slot, :], shifted[:, slot, :], ACT.Exp).then_inc(s["p_ready"], 1)
                steps(act, 4, over_edges)
                act.wait_ge(s["var_ready"], layer + 1)
                act.activation(std[:, :], var_eps[:, :], ACT.Sqrt).then_inc(s["std_ready"], 1)

            with too_many(act):
                for layer in range(LAYERS):
                    with act.Fori(0, T) as t:
                        act.wait_ge(sa["xt_ps"], t + (layer * T + 2))
                        act.activation(all_xT[:, :, bass.ds(t * P, P)],
                                       PS[:, 6, 0:D].rearrange("p (h n) -> p h n", h=H), ACT.Copy).then_inc(sa["xt_sb"], 1)
                    with act.Fori(0, T) as t:
                        act.wait_ge(sa["q_ps"], t + (layer * T + 1))
                        act.activation(one_qT[:, :, :], PS[:, 6, 0:D].rearrange("p (h n) -> p h n", h=H),
                                       ACT.Copy).then_inc(sa["q_sb"], 1)
                        act.wait_ge(sa["neg_topped"], t + (layer * T + 1))
                        act.activation(all_prob, PS[:, 0:4, :].rearrange("p b n -> p (b n)"), ACT.Exp,
                                       bias=row_neg_top[:, :], accum_out=row_total[:, :]).then_inc(sa["exped"], 1)
                        for c in (1, 3):
                            act.wait_ge(sa["t_ps"], t * 4 + (layer * T * 4 + c + 1))
                            act.activation(all_probT[:, 4 * c:4 * c + 4, :],
                                           PS[:, 5, :].rearrange("p (k n) -> p k n", k=4), ACT.Copy).then_inc(sa["t_act"], 1)
                        act.wait_ge(sa["y_ps"], t + (layer * T + 1))
                        act.activation(y_sb[:, :, :], PS[:, 7, 0:D].rearrange("p (h n) -> p h n", h=H),
                                       ACT.Copy).then_inc(sa["y_sb"], 1)
                    act.wait_ge(sa["var_ready"], layer + 1)
                    act.activation(std[:, :], var_eps[:, :], ACT.Sqrt).then_inc(sa["std_ready"], 1)

        @block.vector
        def _(dve):
            chains = {"c": 0}

            def chain(op):
                op.then_inc(s["c"], 1)
                chains["c"] += 1

            def chained():
                dve.wait_ge(s["c"], chains["c"])

            def moments(s, layer):
                dve.tensor_tensor(mean2[:, :], bn[:, :, 1], bn[:, :, 4], ALU.add).then_inc(s["ln"], 1)
                dve.tensor_tensor(gap[:, :], bn[:, :, 1], bn[:, :, 4], ALU.subtract).then_inc(s["ln"], 1)
                dve.tensor_tensor(m2[:, :], bn[:, :, 2], bn[:, :, 5], ALU.add).then_inc(s["ln"], 1)
                dve.wait_ge(s["ln"], 6 * layer + 3)
                dve.tensor_scalar(mean[:, :], mean2[:, :], 0.5, None, ALU.mult).then_inc(s["ln"], 1)
                dve.scalar_tensor_tensor(out=gap2[:, :], in0=gap[:, :], scalar=0.25, in1=gap[:, :],
                                         op0=ALU.mult, op1=ALU.mult).then_inc(s["ln"], 1)
                dve.tensor_scalar(m2e[:, :], m2[:, :], 1.0 / D, EPS, ALU.mult, ALU.add).then_inc(s["ln"], 1)
                dve.wait_ge(s["ln"], 6 * layer + 6)
                dve.tensor_tensor(var_eps[:, :], m2e[:, :], gap2[:, :], ALU.add).then_inc(s["var_ready"], 1)
                dve.wait_ge(s["std_ready"], layer + 1)
                dve.reciprocal(rstd[:, :], std[:, :]).then_inc(s["rstd_ready"], 1)
                dve.wait_ge(s["rstd_ready"], layer + 1)

            dve.memset(started[:, 0:1], 0.0).then_inc(s["res"], 1)
            dve.wait_ge(s["consts"], 10)
            chain(dve.tensor_scalar(row_lo[:, :], row[:, :], G - 1, None, ALU.bitwise_and))
            chained()
            chain(dve.tensor_scalar(row_exp[:, :], row_lo[:, :], 127 + 9, None, ALU.add))
            chained()
            chain(dve.tensor_scalar(row_pow[:, :], row_exp[:, :], 23, None, ALU.logical_shift_left))
            chained()
            dve.tensor_scalar(pack[:, :], group[:, :], row_pow[:, :].bitcast(F32), None, ALU.mult).then_inc(s["dc"], 1)

            words = PS[:, 0:4, :].rearrange("p b (t w) -> p (b t) w", w=NW)
            dve.wait_ge(s["packed"], 1)
            chain(dve.scalar_tensor_tensor(out=key[:, :, :], in0=words, scalar=0.0, in1=iota_w[:, None, :].to_broadcast([P, T, NW]),
                                           op0=ALU.is_gt, op1=ALU.mult))
            chained()
            chain(dve.scalar_tensor_tensor(out=key[:, :, :], in0=key[:, :, :], scalar=65536.0, in1=words,
                                           op0=ALU.mult, op1=ALU.add))
            chained()
            for t in range(T):
                chain(dve.max(top_words[:, t, 0:8], key[:, t, :]))
            chained()
            for t in range(T):
                chain(dve.match_replace(out=key[:, t, :], in_to_replace=top_words[:, t, 0:8],
                                        in_values=key[:, t, :], imm_value=0.0))
            chained()
            for t in range(T):
                chain(dve.max(top_words[:, t, 8:16], key[:, t, :]))
            chained()
            chain(dve.tensor_copy(top_u[:, :, :], top_words[:, :, :]))
            chained()
            chain(dve.tensor_scalar(word_u[:, :, :], top_u[:, :, :], 16, None, ALU.logical_shift_right))
            chain(dve.tensor_scalar(bits_u[:, :, :], top_u[:, :, :], 0xFFFF, None, ALU.bitwise_and))
            chained()
            chain(dve.tensor_scalar(base[:, :, :], word_u[:, :, :], float(G), 1.0 - 127.0, ALU.mult, ALU.add))
            chain(dve.tensor_copy(bits_f[:, :, :], bits_u[:, :, :]))
            chained()
            chain(dve.tensor_scalar(first_e[:, :, :], bits_f[:, :, :].bitcast(U32), 23, None, ALU.logical_shift_right))
            chain(dve.tensor_scalar(first_p[:, :, :].bitcast(U32), bits_f[:, :, :].bitcast(U32), 0x7F800000, None,
                                    ALU.bitwise_and))
            chained()
            chain(dve.tensor_tensor(rest[:, :, :], bits_f[:, :, :], first_p[:, :, :], ALU.subtract))
            chain(dve.tensor_tensor(code1[:, :, :], first_e[:, :, :], base[:, :, :], ALU.add))
            chained()
            chain(dve.tensor_scalar(second_e[:, :, :], rest[:, :, :].bitcast(U32), 23, None, ALU.logical_shift_right))
            chain(dve.tensor_scalar(second_p[:, :, :].bitcast(U32), rest[:, :, :].bitcast(U32), 0x7F800000, None,
                                    ALU.bitwise_and))
            chain(dve.scalar_tensor_tensor(out=codes[:, :, 0:K], in0=bits_f[:, :, :], scalar=0.0, in1=code1[:, :, :],
                                           op0=ALU.is_gt, op1=ALU.mult))
            chained()
            chain(dve.tensor_tensor(rest2[:, :, :], rest[:, :, :], second_p[:, :, :], ALU.subtract))
            chain(dve.tensor_tensor(code2[:, :, :], second_e[:, :, :], base[:, :, :], ALU.add))
            chained()
            chain(dve.scalar_tensor_tensor(out=codes[:, :, K:2 * K], in0=rest[:, :, :], scalar=0.0,
                                           in1=code2[:, :, :], op0=ALU.is_gt, op1=ALU.mult))
            chained()
            for t in range(T):
                chain(dve.max(nbr[:, t, 0:8], codes[:, t, :]))
            chained()
            for t in range(T):
                chain(dve.match_replace(out=codes[:, t, :], in_to_replace=nbr[:, t, 0:8],
                                        in_values=codes[:, t, :], imm_value=0.0))
            chained()
            for t in range(T):
                chain(dve.max(nbr[:, t, 8:16], codes[:, t, :]))
            chained()
            chain(dve.tensor_scalar(picked[:, :, 0, :], nbr[:, :, :], 0.0, None, ALU.is_gt))
            chain(dve.tensor_scalar(no_slot[:, :, :], nbr[:, :, :], 0.0, -NO_EDGE, ALU.is_equal, ALU.mult))
            chained()
            dve.reduce_sum(deg[:, :], picked[:, :, 0, :], axis=AX).then_inc(s["nbrs"], 1)
            chain(dve.tensor_copy(per_query[:, :, 0:K], nbr[:, :, :]))
            chain(dve.tensor_copy(per_query[:, :, K], row_f[:, :].to_broadcast([P, T])))
            dve.wait_ge(s["off_ps"], 1)
            chain(dve.tensor_copy(off[:, :], PS[:, 6, 0:T]))
            chain(dve.tensor_copy(per_query[:, :, K + 1], PS[:, 6, 0:T]))
            chain(dve.reduce_max(count[:, :], PS[:, 6, T:2 * T], axis=AX))
            chained()
            chain(dve.tensor_tensor(end[:, :], off[:, :], deg[:, :], ALU.add))
            chained()

            def own_of(v, g, u):
                t, slot, _ = at(v, g, u, 0)
                need(dve, "own_ready", t)
                dve.tensor_scalar(step[:, :], iota[:, :], off[:, bass.ds(t, 1)], None, ALU.is_ge).then_inc(s["listed"], 1)
                dve.wait_ge(s["listed"], t + 1)
                dve.scalar_tensor_tensor(out=tile(own, t), in0=iota[:, :], scalar=end[:, bass.ds(t, 1)], in1=step[:, :],
                                         op0=ALU.is_lt, op1=ALU.mult).then_inc(s["own_ready"], 1)
            steps(dve, 0, own_of)
            dve.wait_ge(s["l_ps"], 1)
            chain(dve.tensor_copy(L[:, :, :, :],
                                  PS[:, 4:6, :].rearrange("p b (t l) -> p (b t) l", l=LP)[:, :, 0:U * LR]
                                  .rearrange("p t (u l) -> p t u l", u=U)))
            chained()
            chain(dve.tensor_tensor(k_of[:, :, :], iota_e[:, None, :].to_broadcast([P, T, U]), L[:, :, :, K + 1],
                                    ALU.subtract))
            chained()
            kk = k_hot[:, :, :, :].rearrange("p t u k -> p (t u) k")
            chain(dve.tensor_tensor(kk, iota_k[:, None, :].to_broadcast([P, T * U, K]),
                                    k_of[:, :, :].rearrange("p t u -> p (t u)")[:, :, None].to_broadcast([P, T * U, K]),
                                    ALU.is_equal))
            chained()
            chain(dve.tensor_tensor(picked[:, :, :, :], k_hot[:, :, :, :], L[:, :, :, 0:K], ALU.mult))
            chained()
            chain(dve.reduce_sum(code_e[:, :, :], picked[:, :, :, :], axis=AX))
            chained()
            dve.tensor_scalar(key_row[:, :, :], code_e[:, :, :], 1.0, 0.0, ALU.subtract, ALU.max).then_inc(s["listed_e"], 1)

            def own_t_of(v, g, u):
                t, slot, _ = at(v, g, u, 0)
                for n in range(U):
                    last = dve.tensor_scalar(own_t[:, bass.ds(t, 1), n, :].rearrange("p a n -> p (a n)"),
                                             iota[:, 1:P + 1],
                                             L[:, bass.ds(t, 1), n, K].rearrange("p a -> p (a)"), None, ALU.is_equal)
                last.then_inc(s["own_t_ready"], 1)
            steps(dve, 0, own_t_of)
            chain(dve.tensor_scalar(over[:, 0:1], count[:, :], float(E), None, ALU.subtract))
            chain(dve.reduce_max(over[:, 1:2], rest2[:, :, :].rearrange("p t k -> p (t k)"), axis=AX))
            chain(dve.reduce_max(over[:, 2:3], top_words[:, :, K - 1], axis=AX))
            chain(dve.reduce_max(over[:, 3:4], nbr[:, :, K - 1], axis=AX))
            chained()
            chain(dve.reduce_max(over1[:, :], over[:, :], axis=AX))
            chained()
            dve.tensor_scalar(over2[:, :], over1[:, :], 0.0, None, ALU.is_gt).then_inc(s["over_ready"], 1)

            for layer in range(LAYERS):
                if layer == LAYERS - 1:
                    dve.wait_ge(s["flag_ps"], 1)
                    dve.tensor_copy(over_i[:, :], PS[:, 0, 0:1]).then_inc(s["flag"], 1)

                def over_edges(v, g, u):
                    if (now := at(v, g, u, 1)) is not None:
                        t, slot, r = now
                        dve.wait_ge(s["qe_ready"], t + (layer * T + 1))
                        dve.wait_ge(gathered[slot], r * (16 * U) + (layer * (T // RING) + 1) * 16 * U)
                        for n in range(U):
                            dve.tensor_tensor_reduce(
                                out=prod[:, n, :], in0=PS[:, 2 * (slot % 2) + n // 2, D * (n % 2):D * (n % 2) + D],
                                in1=xg[:, slot, n, :], op0=ALU.mult, op1=ALU.add, scale=1.0, scalar=0.0,
                                accum_out=score[:, slot, n:n + 1]).then_inc(s["s_done"], 1)
                    if (now := at(v, g, u, 4)) is not None:
                        t, slot, r = now
                        dve.wait_ge(s["totalled"], t + (layer * T + 1))
                        dve.reciprocal(inv[:, slot, :], total[:, slot, :]).then_inc(s["inved"], 1)
                    if (now := at(v, g, u, 1)) is not None:
                        t, slot, r = now
                        dve.wait_ge(s["s_done"], t * U + (layer * T + 1) * U)
                        dve.tensor_tensor(score_k[:, slot, :, :],
                                          k_hot[:, bass.ds(t, 1), :, :].rearrange("p a u k -> p (a u) k"),
                                          score[:, slot, :, None].to_broadcast([P, U, K]), ALU.mult).then_inc(s["sk_in"], 1)
                    if (now := at(v, g, u, 2)) is not None:
                        t, slot, r = now
                        dve.wait_ge(s["sk_ready"], t + (layer * T + 1))
                        need(dve, "totalled", t + (layer * T - 1))
                        dve.tensor_tensor(masked[:, slot % 2, :], tile(no_slot, t), PS[:, 4 + slot % 2, 0:K],
                                          ALU.subtract).then_inc(s["mask_done"], 1)
                        dve.wait_ge(s["mask_done"], t + (layer * T + 1))
                        dve.tensor_reduce(out=neg_top[:, slot % 2, :], in_=masked[:, slot % 2, :], axis=AX,
                                          op=ALU.min).then_inc(s["maxed"], 1)
                    if (now := at(v, g, u, 4)) is not None:
                        t, slot, r = now
                        dve.wait_ge(s["o_ready"], t + (layer * T + 1))
                        dve.wait_ge(s["inved"], t + (layer * T + 1))
                        dve.scalar_tensor_tensor(out=tile(X[layer + 1], t), in0=PS[:, 7, 0:D], scalar=inv[:, slot, :],
                                                 in1=tile(X[layer], t), op0=ALU.mult, op1=ALU.add).then_inc(s["res"], 1)
                    if (now := at(v, g, u, 2)) is not None:
                        t, slot, r = now
                        dve.wait_ge(s["me_ready"], t + (layer * T + 1))
                        dve.tensor_tensor(shifted[:, slot, :], score[:, slot, :], PS[:, 4 + slot % 2, 2 * K:2 * K + U],
                                          ALU.add).then_inc(s["ds_ready"], 1)
                    if (now := at(v, g, u, 4)) is not None:
                        t, slot, r = now
                        dve.wait_ge(s["res"], t + (layer * T + 2))
                        dve.memset(started[:, 1:2], 0.0).then_inc(s["dc"], 1)
                        dve.bn_stats(tile(bn, t), tile(X[layer + 1], t)).then_inc(s["bn_done"], 1)
                    if (now := at(v, g, u, 2)) is not None:
                        t, slot, r = now
                        dve.wait_ge(s["p_ready"], t + (layer * T + 1))
                        for n in range(U):
                            dve.tensor_scalar(weight[:, slot, n, :], own_tf[:, slot, n, :], prob[:, slot, n:n + 1], None,
                                              ALU.mult).then_inc(s["a_ready"], 1)
                steps(dve, 4, over_edges)

                dve.wait_ge(s["bn_done"], T * (layer + 1))
                moments(s, layer)

                def normalise(v, g, u):
                    t, slot, _ = at(v, g, u, 0)
                    xn = tile(X[layer + 1], t)
                    dve.tensor_scalar(xn, xn, mean[:, bass.ds(t, 1)], rstd[:, bass.ds(t, 1)],
                                      ALU.subtract, ALU.mult).then_inc(s["normed"], 1)
                steps(dve, 0, normalise)

            with too_many(dve):
                for c, n in enumerate(("xt_ps", "xt_sb", "res", "kept")):
                    dve.memset(started[:, 2 + c:3 + c], 0.0).then_inc(sa[n], 1)
                for layer in range(LAYERS):
                    with dve.Fori(0, T) as t:
                        dve.tensor_scalar(not_adj[:, :, :], adj_words[:, :, bass.ds(t * (P // 4), P // 4)], 0x01010101,
                                          None, ALU.bitwise_xor).then_inc(sa["slab"], 1)
                        dve.wait_ge(sa["scored"], t + (layer * T + 1))
                        dve.reduce_max(row_top[:, :], PS[:, 0:4, :].rearrange("p b n -> p (b n)"),
                                       axis=AX).then_inc(sa["topped"], 1)
                        dve.wait_ge(sa["topped"], t + (layer * T + 1))
                        dve.tensor_scalar(row_neg_top[:, :], row_top[:, :], -1.0, None, ALU.mult).then_inc(sa["neg_topped"], 1)
                        dve.tensor_scalar(row_has[:, :], row_top[:, :], NO_EDGE / 2, None, ALU.is_gt).then_inc(sa["has"], 1)
                        dve.wait_ge(sa["exped"], t + (layer * T + 1))
                        dve.reciprocal(row_inv[:, :], row_total[:, :]).then_inc(sa["inved"], 1)
                        dve.wait_ge(sa["inved"], t + (layer * T + 1))
                        dve.tensor_tensor(row_scale[:, :], row_inv[:, :], row_has[:, :], ALU.mult).then_inc(sa["scaled"], 1)
                        for c in (0, 2):
                            dve.wait_ge(sa["t_ps"], t * 4 + (layer * T * 4 + c + 1))
                            dve.tensor_copy(all_probT[:, 4 * c:4 * c + 4, :],
                                            PS[:, 4, :].rearrange("p (k n) -> p k n", k=4)).then_inc(sa["t_dve"], 1)
                        dve.wait_ge(sa["o_ps"], t + (layer * T + 1))
                        dve.wait_ge(sa["kept"], t + (layer * T + 1))
                        dve.scalar_tensor_tensor(out=new_row[:, :], in0=PS[:, 6, D:2 * D], scalar=row_scale[:, :],
                                                 in1=tile(X[layer], t), op0=ALU.mult, op1=ALU.add).then_inc(sa["res"], 1)
                        dve.wait_ge(sa["res"], t + (layer * T + 2))
                        dve.bn_stats(bn_row[:, :], new_row[:, :]).then_inc(sa["stat"], 1)
                        dve.wait_ge(sa["stat"], t + (layer * T + 1))
                        dve.tensor_copy(tile(bn, t), bn_row[:, :]).then_inc(sa["moved"], 1)
                    dve.wait_ge(sa["moved"], T * (layer + 1))
                    moments(sa, layer)
                    dve.wait_ge(sa["kept"], T * (layer + 1) + 1)
                    with dve.Fori(0, T) as t:
                        xn = tile(X[layer + 1], t)
                        dve.tensor_scalar(xn, xn, mean[:, bass.ds(t, 1)], rstd[:, bass.ds(t, 1)],
                                          ALU.subtract, ALU.mult).then_inc(sa["normed"], 1)

        @block.tensor
        def _(pe):
            pe.wait_ge(s["dc"], 1)
            for j in range(T):
                if j % 4 == 0:
                    pe.wait_ge(a_in[j // 4], 16)
                for t in range(T):
                    last = nc.tensor.matmul(PS[:, t // 4, (t % 4) * NW + j * WT:(t % 4) * NW + (j + 1) * WT],
                                            adj_words[:, j, t * (P // 4):(t + 1) * (P // 4)].bitcast(FP8), pack[:, :],
                                            start=True, stop=True)
            last.then_inc(s["packed"], 1)
            pe.wait_ge(s["w_in"], 16 * 3 * LAYERS)
            for n in range(LAYERS):
                if n > 0:
                    pe.wait_ge(s["m_sb"], 2 * n - 1)
                for h in range(H):
                    for e in range(H):
                        last = nc.tensor.matmul(PS[:, 6, h * D:h * D + D], W[:, n, 0, e, h * P:h * P + P], W[:, n, 1, e, :],
                                                start=(e == 0), stop=(e == H - 1))
                last.then_inc(s["m_ps"], 1)
                if n > 0:
                    pe.wait_ge(s["m_sb"], 2 * n)
                for h in range(H):
                    for e in range(H):
                        last = nc.tensor.transpose(PS[:, 7, h * D + e * P:h * D + e * P + P],
                                                   W[:, n, 2, e, h * P:h * P + P], ident[:, :])
                last.then_inc(s["m_ps"], 1)
            pe.wait_ge(s["m_sb"], 2 * LAYERS)

            for layer in range(LAYERS):
                def project(v, g, u):
                    if (now := at(v, g, u, 0)) is not None:
                        t, slot, _ = now
                        pe.wait_ge(s["staged"], t + (layer * T + 1))
                        need(pe, "xt_sb", t + (layer * T - 1))
                        for h in range(H):
                            last = nc.tensor.transpose(PS[:, 4 + slot % 2, h * P:h * P + P],
                                                       stage[:, slot, h * P:h * P + P], ident[:, :])
                        last.then_inc(s["xt_ps"], 1)
                    if (now := at(v, g, u, 1)) is not None:
                        t, slot, _ = now
                        pe.wait_ge(s["xt_sb"], t + (layer * T + 1))
                        need(pe, "q_sb", t + (layer * T - 1))
                        for h in range(H):
                            last = nc.tensor.matmul(PS[:, 6 + slot % 2, 0:D], xt[:, slot, h, :], M[:, layer, h, :],
                                                    start=(h == 0), stop=(h == H - 1))
                        last.then_inc(s["q_ps"], 1)
                steps(pe, 1, project)
                pe.wait_ge(s["q_sb"], T * (layer + 1))

                if layer == 0:
                    pe.wait_ge(s["nbrs"], 1)
                    nc.tensor.matmul(PS[:, 6, 0:T], before[:, :], deg[:, :], start=True, stop=True)
                    nc.tensor.matmul(PS[:, 6, T:2 * T], ones[:, :], deg[:, :], start=True, stop=True).then_inc(s["off_ps"], 1)
                    for t in range(T):
                        pe.wait_ge(s["own_ready"], t + 1)
                        for n in range(U):
                            at_l = (t % 8) * LP + n * LR
                            last = nc.tensor.matmul(PS[:, 4 + t // 8, at_l:at_l + LR], own[:, t, n * P:n * P + P],
                                                    per_query[:, t, :], start=True, stop=True)
                    last.then_inc(s["l_ps"], 1)
                    pe.wait_ge(s["listed_e"], 1)
                if layer == LAYERS - 1:
                    pe.wait_ge(s["over_ready"], 1)
                    pe.wait_ge(s["s_done"], layer * T * U)
                    nc.tensor.matmul(PS[:, 0, 0:1], ones[:, :], over2[:, :], start=True, stop=True).then_inc(s["flag_ps"], 1)
                    pe.wait_ge(s["flag"], 1)

                def over_edges(v, g, u):
                    if (now := at(v, g, u, 1)) is not None:
                        t, slot, _ = now
                        pe.wait_ge(s["own_f_ready"], t + (layer * T + 1))
                        need(pe, "s_done", t * U + (layer * T - 1) * U)
                        for n in range(U):
                            last = nc.tensor.matmul(PS[:, 2 * (slot % 2) + n // 2, D * (n % 2):D * (n % 2) + D],
                                                    own_f[:, slot, n * P:n * P + P], tile(Q, t), start=True, stop=True)
                        last.then_inc(s["qe_ready"], 1)
                    if (now := at(v, g, u, 4)) is not None:
                        t, slot, _ = now
                        pe.wait_ge(s["y_sb_ready"], t + (layer * T + 1))
                        pe.wait_ge(s["res"], t + (layer * T + 1))
                        for h in range(H):
                            last = nc.tensor.matmul(PS[:, 7, 0:D], y_sb[:, h, :], WvT[:, layer, h, :],
                                                    start=(h == 0), stop=(h == H - 1))
                        last.then_inc(s["o_ready"], 1)
                    if (now := at(v, g, u, 2)) is not None:
                        t, slot, _ = now
                        pe.wait_ge(s["sk_in"], t + (layer * T + 1))
                        pe.wait_ge(s["own_tf_ready"], t + (layer * T + 1))
                        need(pe, "ds_ready", t + (layer * T - 1))
                        for n in range(U):
                            last = nc.tensor.matmul(PS[:, 4 + slot % 2, 0:K], own_tf[:, slot, n, :], score_k[:, slot, n, :],
                                                    start=(n == 0), stop=(n == U - 1))
                        last.then_inc(s["sk_ready"], 1)
                    if (now := at(v, g, u, 3)) is not None:
                        t, slot, _ = now
                        pe.wait_ge(s["a_ready"], t * U + (layer * T + 1) * U)
                        for h in range(H):
                            for n in range(U):
                                last = nc.tensor.matmul(PS[:, 6, h * P:h * P + P], xg[:, slot, n, h * P:h * P + P],
                                                        weight[:, slot, n, :], start=(n == 0), stop=(n == U - 1))
                        last.then_inc(s["y_ready"], 1)
                    if (now := at(v, g, u, 2)) is not None:
                        t, slot, _ = now
                        pe.wait_ge(s["maxed"], t + (layer * T + 1))
                        for n in range(U):
                            last = nc.tensor.matmul(PS[:, 4 + slot % 2, 2 * K + n:2 * K + n + 1],
                                                    own_f[:, slot, n * P:n * P + P], neg_top[:, slot % 2, :],
                                                    start=True, stop=True)
                        last.then_inc(s["me_ready"], 1)
                steps(pe, 4, over_edges)

            with too_many(pe):
                pe.wait_ge(sa["no_edge"], 1)
                for layer in range(LAYERS):
                    with pe.Fori(0, T) as t:
                        pe.wait_ge(sa["staged"], t + (layer * T + 1))
                        pe.wait_ge(sa["xt_sb"], t + (layer * T + 1))
                        for h in range(H):
                            last = nc.tensor.transpose(PS[:, 6, h * P:h * P + P], one_row[:, h * P:h * P + P], ident[:, :])
                        last.then_inc(sa["xt_ps"], 1)
                    pe.wait_ge(sa["xt_sb"], T * (layer + 1) + 1)
                    with pe.Fori(0, T) as t:
                        pe.wait_ge(sa["res"], t + (layer * T + 1))
                        pe.wait_ge(sa["slab"], t + (layer * T + 1))
                        for h in range(H):
                            for e in range(H):
                                last = nc.tensor.matmul(PS[:, 6, h * P:h * P + P], M[:, layer, e, h * P:h * P + P],
                                                        all_xT[:, e, bass.ds(t * P, P)], start=(e == 0), stop=(e == H - 1))
                        last.then_inc(sa["q_ps"], 1)
                        for j in range(T):
                            nc.tensor.matmul(PS[:, j // 4, (j % 4) * P:(j % 4) * P + P], not_adj[:, j, :].bitcast(FP8),
                                             no_edge_ident[:, :], start=(j % 4 == 0), stop=False, skip_group_check=True)
                        pe.wait_ge(sa["q_sb"], t + (layer * T + 1))
                        for h in range(H):
                            for c in range(4):
                                last = nc.tensor.matmul(PS[:, c, :], one_qT[:, h, :], all_xT[:, h, c * BANK:c * BANK + BANK],
                                                        start=False, stop=(h == H - 1), skip_group_check=True)
                        last.then_inc(sa["scored"], 1)
                        pe.wait_ge(sa["exped"], t + (layer * T + 1))
                        for c in range(4):
                            if c == 2:
                                pe.wait_ge(sa["t_dve"], t * 2 + (layer * T * 2 + 1))
                            if c == 3:
                                pe.wait_ge(sa["t_act"], t * 2 + (layer * T * 2 + 1))
                            for k in range(4):
                                j = 4 * c + k
                                last = nc.tensor.transpose(PS[:, 4 + c % 2, k * P:k * P + P], all_prob[:, j * P:j * P + P],
                                                           ident[:, :])
                            last.then_inc(sa["t_ps"], 1)
                        pe.wait_ge(sa["t_dve"], t * 2 + (layer * T * 2 + 2))
                        pe.wait_ge(sa["t_act"], t * 2 + (layer * T * 2 + 2))
                        for h in range(H):
                            for j in range(T):
                                last = nc.tensor.matmul(PS[:, 7, h * P:h * P + P], X[layer][:, j, h * P:h * P + P],
                                                        all_probT[:, j, :], start=(j == 0), stop=(j == T - 1))
                        last.then_inc(sa["y_ps"], 1)
                        pe.wait_ge(sa["y_sb"], t + (layer * T + 1))
                        for h in range(H):
                            last = nc.tensor.matmul(PS[:, 6, D:2 * D], y_sb[:, h, :], WvT[:, layer, h, :],
                                                    start=(h == 0), stop=(h == H - 1))
                        last.then_inc(sa["o_ps"], 1)


def kernel(**inputs):
    import numpy as np
    import concourse.bacc as bacc
    from concourse.bass_utils import run_bass_kernel_spmd as run

    nc = bacc.Bacc("TRN2", target_bir_lowering=False, num_devices=1)
    arrays, ap = {}, {}
    for name, value in inputs.items():
        a = np.ascontiguousarray(value)
        if a.dtype == np.bool_:
            a = a.view(np.uint32)
        arrays[f"in_{name}"] = a
        ap[name] = nc.dram_tensor(f"in_{name}", a.shape, mybir.dt.from_np(a.dtype), kind="ExternalInput").ap()
    out = nc.dram_tensor("out", (N, D), F32, kind="ExternalOutput").ap()
    w = {k: [ap[f"L{n}_gnn_W{k}"] for n in range(LAYERS)] for k in "qkv"}
    edges_and_dense(nc, ap["x"], ap["adj"], w["q"], w["k"], w["v"], out)
    return run(nc, [arrays], core_ids=[0]).results[0]["out"]
```

```python
import concourse.bass as bass
from concourse import mybir
from contextlib import ExitStack

F32 = mybir.dt.float32
F16 = mybir.dt.float16
BF16 = mybir.dt.bfloat16
FP8 = mybir.dt.float8e4
U32 = mybir.dt.uint32
I32 = mybir.dt.int32
ALU = mybir.AluOpType
ACT = mybir.ActivationFunctionType
AX = mybir.AxisListType.X

P = 128
N = 2048
D = 256
T = N // P
H = D // P
LAYERS = 2
EPS = 1e-5
BANK = 512
TRUE_AS_FP8 = 2.0 ** -9
NO_EDGE = -(2.0 ** 100)

G = 16
NW = N // G
WT = P // G
C = 4
WC = NW // C
KC = 8
K = 16
U = 3
E = U * P
PAIRS = T // 2
RING = 8
FIRST = 7
ASKED = (None, None, None, 7, 8, 9, 10, 11, 12, 13), (14, 15)
STEPS = len(ASKED[0])
SHIFT_AT = 1
OFFSETS_AT = FIRST + 2
PACK_AT = (1, 2)
LR = K + 2
LISTS = 2
LP = 64
S3 = 3


def edges_and_dense(nc, x, adj, wq, wk, wv, out):
    ctx = ExitStack()
    with ctx:
        def sb(name, shape, dt=F32):
            return ctx.enter_context(nc.sbuf_tensor(name, shape, dt))

        def sem(name):
            return ctx.enter_context(nc.semaphore(name))

        x1_dram = nc.dram_tensor("x1_rows", (N, D), F32, kind="Internal").ap()

        X0 = sb("X0", [P, T, D])
        X1 = sb("X1", [P, T, D])
        X = [X0, X1, X0]
        adj_words = sb("adj_words", [P, T, N // 4], U32)
        W = sb("W", [P, LAYERS, 3, H, D])
        M = sb("M", [P, LAYERS, H, D])
        WvT = sb("WvT", [P, LAYERS, H, D])
        ident = sb("ident", [P, P])
        bn = sb("bn", [P, T, 6])
        bn_pair = sb("bn_pair", [P, 2, 6])
        moment = sb("moment", [P, 2, 2])
        var_pair, less_half, guess, near = (sb(n, [P, 2]) for n in "var_pair less_half guess near".split())
        mean2, gap, m2, mean, gap2, m2e, var_eps, std, rstd = (
            sb(n, [P, T]) for n in "mean2 gap m2 mean gap2 m2e var_eps std rstd".split())
        started = sb("started", [P, 8])

        ones = sb("ones", [P, P])
        before = sb("before", [P, P])
        iota = sb("iota", [P, E], F16)
        ident_h = sb("ident_h", [P, P], F16)
        minus = sb("minus", [P, P], BF16)
        iota_w = sb("iota_w", [P, NW])
        iota_k = sb("iota_k", [P, K])
        iota_e = sb("iota_e", [P, U])
        row = sb("row", [P, 1], I32)
        row_lo = sb("row_lo", [P, 1], I32)
        row_exp = sb("row_exp", [P, 1], I32)
        row_pow = sb("row_pow", [P, 1], I32)
        row_f = sb("row_f", [P, 1])
        group = sb("group", [P, WT])
        pack = sb("pack", [P, WT], BF16)
        top_words = sb("top_words", [P, C, T, KC])
        top_u, word_u, bits_u, first_e, second_e = (
            sb(n, [P, T, KC], U32) for n in "top_u word_u bits_u first_e second_e".split())
        bits_f, first_p, rest, second_p, base, code1, code2 = (
            sb(n, [P, T, KC]) for n in "bits_f first_p rest second_p base code1 code2".split())
        rest2 = sb("rest2", [P, C, T, KC])
        nbr = sb("nbr", [P, T, K])
        deg = sb("deg", [P, T])
        start_half = sb("start_half", [P, T])
        shift = sb("shift", [P, T])
        half = sb("half", [P, T])
        count = sb("count", [P, 1])
        over = sb("over", [P, 4])
        over1 = sb("over1", [P, 1])
        over2 = sb("over2", [P, 1])
        over_i = sb("over_i", [P, 1], I32)
        per_query = sb("per_query", [P, T, LR], F16)
        dist = sb("dist", [P, 4, E], F16)
        own = sb("own", [P, T, E], F16)
        own_t = sb("own_t", [P, T, U, P], F16)
        L = sb("L", [P, T, U, LR])
        k_of = sb("k_of", [P, T, U])
        k_hot = sb("k_hot", [P, T, U, K], BF16)
        picked = sb("picked", [P, T, U, K])
        code_e = sb("code_e", [P, T, U])
        key_row = sb("key_row", [P, T, U], U32)
        no_slot = sb("no_slot", [P, T, K], BF16)

        Q = sb("Q", [P, T, S3, D], BF16)
        xt = sb("xt", [P, 2, H, P])
        xg = sb("xg", [P, RING, U, D])
        key = xg[:, 0:2, :, :].rearrange("p r u d -> p (r u d)")[:, 0:2 * T * WC].rearrange(
            "p (c t w) -> p c t w", c=2, t=T)
        codes = xg[:, 2:4, :, :].rearrange("p r u d -> p (r u d)")[:, 0:T * C * 2 * KC].rearrange(
            "p (t c s k) -> p t c s k", t=T, c=C, s=2)
        prod = sb("prod", [P, 2, U, D])
        neg_score = sb("neg_score", [P, 2, 2 * U])
        s_rest = sb("s_rest", [P, 2 * U])
        s_part = sb("s_part", [P, 2 * U, S3], BF16)
        score_k = sb("score_k", [P, 2 * U, S3, K], BF16)
        neg_top = sb("neg_top", [P, 2])
        top_rest = sb("top_rest", [P, 2])
        top_part = sb("top_part", [P, 2, S3], BF16)
        exps = sb("exps", [P, 2, K])
        total = sb("total", [P, T])
        inv = sb("inv", [P, T])
        edge_top = sb("edge_top", [P, 2 * U])
        shifted = sb("shifted", [P, 2 * U])
        prob = sb("prob", [P, 2 * U])
        weight = sb("weight", [P, 2, U, P])
        y_sb = sb("y_sb", [P, 2, H, P])

        all_xT = Q[:, :, :, :].rearrange("p t s d -> p (t s d)").bitcast(F32)[:, 0:H * N].rearrange(
            "p (h n) -> p h n", h=H)
        all_prob = own[:, :, :].rearrange("p t e -> p (t e)").bitcast(F32)[:, 0:N]
        all_probT = own_t[:, :, :, :].rearrange("p t u q -> p (t u q)").bitcast(F32)[:, 0:N].rearrange(
            "p (t q) -> p t q", t=T)
        not_adj = sb("not_adj", [P, T, P // 4], U32)
        no_edge_ident = sb("no_edge_ident", [P, P], BF16)
        one_row = sb("one_row", [P, D])
        one_qT = sb("one_qT", [P, H, P])
        new_row = sb("new_row", [P, D])
        bn_row = sb("bn_row", [P, 6])
        row_top, row_neg_top, row_has, row_total, row_inv, row_scale = (
            sb(n, [P, 1]) for n in "row_top row_neg_top row_has row_total row_inv row_scale".split())

        PS = ctx.enter_context(nc.psum_tensor("PS", [P, 8, BANK], F32))

        names = """w_first w_in x_in x_rest_in memsets consts dc packed chained nbrs off_ps off_read shifts dist_ready
            own_ready own_t_ps own_t_act own_t_dve l_ps listed over_ready flag_ps flag m_ps m_sb xt_ps xt_sb q_ps q_hi q_less_hi
            q_mid q_less_mid q_lo qe_ready s_done sk_in sk_ready topped top_split me_ready ds_ready totalled p_ready a_ready
            y_ready y_sb_ready o_ready stats res normed x1_stored stored""".split()
        s = {n: sem(n) for n in names}
        names = """x_again no_edge_set no_edge staged xt_ps xt_sb q_ps q_sb slab scored topped neg_topped has exped
            t_ps t_act t_dve y_ps y_sb o_ps res stat moved inved scaled ln var_ready std_ready rstd_ready kept
            normed stored""".split()
        sa = {n: sem("all_" + n) for n in names}
        a_in = [sem(f"a_in{c}") for c in range(C)]
        gathered = [sem(f"gathered{c}") for c in range(RING)]
        block = ctx.enter_context(nc.Block())

        def too_many(eng):
            eng.wait_ge(s["flag"], 1)
            return eng.If(eng.value_load(over_i[0:1, 0:1], min_val=0, max_val=P))

        def need(eng, name, value):
            if not isinstance(value, int) or value > 0:
                eng.wait_ge(s[name] if isinstance(name, str) else name, value)

        def tile(ap, t):
            return ap[:, bass.ds(t, 1), :].rearrange("p a d -> p (a d)")

        def expanded(j, n):
            return PS[:, 2 * j + n // 2, n % 2 * D:n % 2 * D + D]

        def halves(bank):
            return PS[:, bank, :].rearrange("p (j d) -> p j d", j=2)

        first_xt = [xt, y_sb]

        def asked(layer, p):
            return ASKED[layer][p] if p < len(ASKED[layer]) else None

        def turned_for(layer, p):
            return asked(layer, p + 1) if layer > 0 or p + 1 < STEPS else asked(1, 0)

        def among(k):
            return 0 <= k < PAIRS

        @block.sync
        def _(sp):
            half_rows = N // 2

            def adjacency(c):
                sp.dma_start(adj_words[:, 4 * c:4 * c + 4, :],
                             adj[512 * c:512 * c + 512, :].rearrange("(t p) n -> p t n", p=P)).then_inc(a_in[c], 16)

            adjacency(0)
            adjacency(1)
            for i, w in enumerate((wq[0], wk[0])):
                sp.dma_start(W[:, 0, i, :, :], w.rearrange("(h p) d -> p h d", p=P)).then_inc(s["w_first"], 16)
            sp.dma_start(X0[:, 0:T // 2, :], x[0:half_rows, :].rearrange("(t p) d -> p t d", p=P)).then_inc(s["x_in"], 16)
            adjacency(2)
            adjacency(3)
            sp.dma_start(X0[:, T // 2:T, :], x[half_rows:N, :].rearrange("(t p) d -> p t d", p=P)).then_inc(s["x_rest_in"], 16)
            for n, i, w in ((0, 2, wv[0]), (1, 0, wq[1]), (1, 1, wk[1]), (1, 2, wv[1])):
                sp.dma_start(W[:, n, i, :, :], w.rearrange("(h p) d -> p h d", p=P)).then_inc(s["w_in"], 16)
            for layer, rows, name in ((0, x1_dram, "x1_stored"), (1, out, "stored")):
                for k in range(PAIRS):
                    sp.wait_ge(s["normed"], T * layer + 2 * (k + 1))
                    sp.dma_start(rows[2 * P * k:2 * P * (k + 1), :].rearrange("(t p) d -> p t d", p=P),
                                 X[layer + 1][:, 2 * k:2 * k + 2, :]).then_inc(s[name], 16)
            sp.wait_ge(s["stored"], 16 * PAIRS)

            with too_many(sp):
                sp.dma_start(X0[:, :, :], x.rearrange("(t p) d -> p t d", p=P)).then_inc(sa["x_again"], 16)
                sp.wait_ge(sa["normed"], LAYERS * T)
                sp.dma_start(out.rearrange("(t p) d -> p t d", p=P), X[LAYERS][:, :, :]).then_inc(sa["stored"], 16)
                sp.wait_ge(sa["stored"], 16)

        @block.gpsimd
        def _(pool):
            pool.memset(ident[:, :], 0.0).then_inc(s["memsets"], 1)
            pool.memset(group[:, :], 1.0).then_inc(s["memsets"], 1)
            pool.memset(before[:, :], 1.0).then_inc(s["memsets"], 1)
            pool.iota(row[:, :], pattern=[[0, 1]], base=0, channel_multiplier=1).then_inc(s["consts"], 1)
            pool.memset(ident_h[:, :], 0.0).then_inc(s["memsets"], 1)
            pool.memset(minus[:, :], 0.0).then_inc(s["memsets"], 1)
            pool.wait_ge(s["memsets"], 5)
            pool.affine_select(out=group[:, :], in_=group[:, :], compare_op=ALU.is_ge, fill=0.0, base=0,
                               pattern=[[-G, WT]], channel_multiplier=1).then_inc(s["memsets"], 1)
            pool.wait_ge(s["memsets"], 6)
            pool.affine_select(out=group[:, :], in_=group[:, :], compare_op=ALU.is_ge, fill=0.0, base=G - 1,
                               pattern=[[G, WT]], channel_multiplier=-1).then_inc(s["consts"], 1)
            pool.affine_select(out=ident[:, :], in_=ident[:, :], compare_op=ALU.not_equal, fill=1.0, base=0,
                               pattern=[[-1, P]], channel_multiplier=1).then_inc(s["consts"], 1)
            pool.affine_select(out=ident_h[:, :], in_=ident_h[:, :], compare_op=ALU.not_equal, fill=1.0, base=0,
                               pattern=[[-1, P]], channel_multiplier=1).then_inc(s["consts"], 1)
            pool.affine_select(out=minus[:, :], in_=minus[:, :], compare_op=ALU.not_equal, fill=-1.0, base=0,
                               pattern=[[-1, P]], channel_multiplier=1).then_inc(s["consts"], 1)
            pool.affine_select(out=before[:, :], in_=before[:, :], compare_op=ALU.is_ge, fill=0.0, base=-1,
                               pattern=[[1, P]], channel_multiplier=-1).then_inc(s["consts"], 1)
            pool.memset(ones[:, :], 1.0).then_inc(s["consts"], 1)
            pool.iota(iota[:, :], pattern=[[1, E]], base=0, channel_multiplier=0,
                      allow_small_or_imprecise_dtypes=True).then_inc(s["consts"], 1)
            pool.iota(iota_w[:, :], pattern=[[1, NW]], base=0, channel_multiplier=0,
                      allow_small_or_imprecise_dtypes=True).then_inc(s["consts"], 1)
            pool.iota(iota_k[:, :], pattern=[[1, K]], base=0, channel_multiplier=0,
                      allow_small_or_imprecise_dtypes=True).then_inc(s["consts"], 1)
            pool.iota(iota_e[:, :], pattern=[[P, U]], base=0, channel_multiplier=1,
                      allow_small_or_imprecise_dtypes=True).then_inc(s["consts"], 1)
            pool.iota(row_f[:, :], pattern=[[0, 1]], base=1, channel_multiplier=1,
                      allow_small_or_imprecise_dtypes=True).then_inc(s["consts"], 1)

            for layer in range(LAYERS):
                rows = x if layer == 0 else x1_dram
                if layer > 0:
                    pool.wait_ge(s["x1_stored"], 16 * PAIRS)
                for t in range(T):
                    if layer == 0 and t % (T // LISTS) == 0:
                        pool.wait_ge(s["listed"], t // (T // LISTS) + 1)
                    need(pool, "y_ready", t + layer * T - RING + 1)
                    for n in range(U):
                        pool.indirect_dma_start(xg[:, t % RING, n, :], None, rows,
                                                bass.IndirectOffsetOnAxis(ap=key_row[:, t, n:n + 1], axis=0),
                                                bounds_check=N - 1, oob_is_err=False).then_inc(gathered[t % RING], 16)

            with too_many(pool):
                pool.memset(no_edge_ident[:, :], 0.0).then_inc(sa["no_edge_set"], 1)
                pool.wait_ge(sa["no_edge_set"], 1)
                pool.affine_select(out=no_edge_ident[:, :], in_=no_edge_ident[:, :], compare_op=ALU.not_equal,
                                   fill=NO_EDGE / TRUE_AS_FP8, base=0, pattern=[[-1, P]],
                                   channel_multiplier=1).then_inc(sa["no_edge"], 1)
                for layer in range(LAYERS):
                    if layer == 0:
                        pool.wait_ge(sa["x_again"], 16)
                    else:
                        pool.wait_ge(sa["normed"], layer * T)
                    with pool.Fori(0, T) as t:
                        pool.wait_ge(sa["xt_ps"], t + (layer * T + 1))
                        pool.tensor_copy(one_row[:, :], tile(X[layer], t)).then_inc(sa["staged"], 1)
                    with pool.Fori(0, T) as t:
                        pool.wait_ge(sa["res"], t + (layer * T + 2))
                        pool.tensor_copy(tile(X[layer + 1], t), new_row[:, :]).then_inc(sa["kept"], 1)

        @block.scalar
        def _(act):
            def weights(n, bank, into, nth):
                act.wait_ge(s["m_ps"], nth)
                act.activation(into[:, n, :, :], PS[:, bank, :].rearrange("p (h d) -> p h d", h=H), ACT.Copy).then_inc(s["m_sb"], 1)

            weights(0, 6, M, 1)
            for i in range(FIRST + 3):
                if i < FIRST:
                    act.wait_ge(s["xt_ps"], i + 1)
                    act.activation(first_xt[i % 2][:, :, :, :], PS[:, 4, :].rearrange("p (j h n) -> p j h n", j=2, h=H),
                                   ACT.Copy).then_inc(s["xt_sb"], 1)
                for lag, part, source, done in ((1, 0, "q_ps", "q_hi"), (2, 1, "q_less_hi", "q_mid"),
                                                (3, 2, "q_less_mid", "q_lo")):
                    k = i - lag
                    if 0 <= k < FIRST:
                        act.wait_ge(s[source], k + 1)
                        act.activation(Q[:, 2 * k:2 * k + 2, part, :], halves(5 + k % 3), ACT.Copy).then_inc(s[done], 1)
            act.wait_ge(s["shifts"], 1)
            for step in range(T + 2):
                if step < T:
                    if step >= 4:
                        act.wait_ge(s["own_ready"], step - 3)
                    act.activation(dist[:, step % 4, :], iota[:, :], ACT.Abs,
                                   bias=shift[:, step:step + 1]).then_inc(s["dist_ready"], 1)
                t = step - 2
                if t >= 0 and t % 2 == 0:
                    act.wait_ge(s["own_t_ps"], t + 1)
                    act.activation(own_t[:, t, :, :],
                                   PS[:, t % 4, 0:E // 2].bitcast(F16).rearrange("p (u n) -> p u n", u=U),
                                   ACT.Copy).then_inc(s["own_t_act"], 1)

            for nth, (n, bank, into) in enumerate(((0, 7, WvT), (1, 6, M), (1, 5, WvT))):
                weights(n, bank, into, nth + 2)

            def rows_turned(z):
                act.wait_ge(s["xt_ps"], z + 1)
                act.activation(xt[:, :, :, :], PS[:, 7, :].rearrange("p (j h n) -> p j h n", j=2, h=H),
                               ACT.Copy).then_inc(s["xt_sb"], 1)

            def query_part(z, part, source, done):
                k = z % PAIRS
                act.wait_ge(s[source], z + 1)
                act.activation(Q[:, 2 * k:2 * k + 2, part, :], halves(7), ACT.Copy).then_inc(s[done], 1)

            def summed(layer, k):
                act.wait_ge(s["y_ready"], layer * T + 2 * k + 2)
                act.activation(y_sb[:, :, :, :], PS[:, 5, :].rearrange("p (j h n) -> p j h n", j=2, h=H),
                               ACT.Copy).then_inc(s["y_sb_ready"], 1)

            for layer in range(LAYERS):
                for p in range(STEPS):
                    if p == PAIRS:
                        summed(layer, p - 1)
                    if (z := asked(layer, p)) is not None:
                        query_part(z, 0, "q_ps", "q_hi")
                        query_part(z, 1, "q_less_hi", "q_mid")
                        query_part(z, 2, "q_less_mid", "q_lo")
                    if among(p):
                        act.wait_ge(s["topped"], layer * PAIRS + p + 1)
                        for j in range(2):
                            act.activation(exps[:, j, :], PS[:, 4, j * K:(j + 1) * K], ACT.Exp, bias=neg_top[:, j:j + 1], scale=-1.0,
                                           accum_out=total[:, 2 * p + j:2 * p + j + 1]).then_inc(s["totalled"], 1)
                    if 0 < p < PAIRS:
                        summed(layer, p - 1)
                    if (z := turned_for(layer, p)) is not None:
                        rows_turned(z)
                    if among(p):
                        act.wait_ge(s["ds_ready"], layer * PAIRS + p + 1)
                        act.activation(prob[:, :], shifted[:, :], ACT.Exp, scale=-1.0).then_inc(s["p_ready"], 1)
                        act.wait_ge(s["p_ready"], layer * PAIRS + p + 1)
                        need(act, "y_ready", layer * T + 2 * p)
                        for j in range(2):
                            for n in range(U):
                                act.activation(weight[:, j, n, :], own_t[:, 2 * p + j, n, :], ACT.Copy,
                                               scale=prob[:, j * U + n:j * U + n + 1]).then_inc(s["a_ready"], 1)

            with too_many(act):
                for layer in range(LAYERS):
                    with act.Fori(0, T) as t:
                        act.wait_ge(sa["xt_ps"], t + (layer * T + 2))
                        act.activation(all_xT[:, :, bass.ds(t * P, P)],
                                       PS[:, 6, 0:D].rearrange("p (h n) -> p h n", h=H), ACT.Copy).then_inc(sa["xt_sb"], 1)
                    with act.Fori(0, T) as t:
                        act.wait_ge(sa["q_ps"], t + (layer * T + 1))
                        act.activation(one_qT[:, :, :], PS[:, 6, 0:D].rearrange("p (h n) -> p h n", h=H),
                                       ACT.Copy).then_inc(sa["q_sb"], 1)
                        act.wait_ge(sa["neg_topped"], t + (layer * T + 1))
                        act.activation(all_prob, PS[:, 0:4, :].rearrange("p b n -> p (b n)"), ACT.Exp,
                                       bias=row_neg_top[:, :], accum_out=row_total[:, :]).then_inc(sa["exped"], 1)
                        for c in (1, 3):
                            act.wait_ge(sa["t_ps"], t * 4 + (layer * T * 4 + c + 1))
                            act.activation(all_probT[:, 4 * c:4 * c + 4, :],
                                           PS[:, 5, :].rearrange("p (k n) -> p k n", k=4), ACT.Copy).then_inc(sa["t_act"], 1)
                        act.wait_ge(sa["y_ps"], t + (layer * T + 1))
                        act.activation(y_sb[:, 0, :, :], PS[:, 7, 0:D].rearrange("p (h n) -> p h n", h=H),
                                       ACT.Copy).then_inc(sa["y_sb"], 1)
                    act.wait_ge(sa["var_ready"], layer + 1)
                    act.activation(std[:, :], var_eps[:, :], ACT.Sqrt).then_inc(sa["std_ready"], 1)

        @block.vector
        def _(dve):
            chains = {"c": 0}

            def chain(op):
                op.then_inc(s["chained"], 1)
                chains["c"] += 1
                return chains["c"]

            def chained(nth=None):
                dve.wait_ge(s["chained"], nth or chains["c"])

            def moments(s, layer):
                dve.tensor_tensor(mean2[:, :], bn[:, :, 1], bn[:, :, 4], ALU.add).then_inc(s["ln"], 1)
                dve.tensor_tensor(gap[:, :], bn[:, :, 1], bn[:, :, 4], ALU.subtract).then_inc(s["ln"], 1)
                dve.tensor_tensor(m2[:, :], bn[:, :, 2], bn[:, :, 5], ALU.add).then_inc(s["ln"], 1)
                dve.wait_ge(s["ln"], 6 * layer + 3)
                dve.tensor_scalar(mean[:, :], mean2[:, :], 0.5, None, ALU.mult).then_inc(s["ln"], 1)
                dve.scalar_tensor_tensor(out=gap2[:, :], in0=gap[:, :], scalar=0.25, in1=gap[:, :],
                                         op0=ALU.mult, op1=ALU.mult).then_inc(s["ln"], 1)
                dve.tensor_scalar(m2e[:, :], m2[:, :], 1.0 / D, EPS, ALU.mult, ALU.add).then_inc(s["ln"], 1)
                dve.wait_ge(s["ln"], 6 * layer + 6)
                dve.tensor_tensor(var_eps[:, :], m2e[:, :], gap2[:, :], ALU.add).then_inc(s["var_ready"], 1)
                dve.wait_ge(s["std_ready"], layer + 1)
                dve.reciprocal(rstd[:, :], std[:, :]).then_inc(s["rstd_ready"], 1)
                dve.wait_ge(s["rstd_ready"], layer + 1)

            dve.memset(started[:, 0:1], 0.0).then_inc(s["res"], 1)
            dve.wait_ge(s["consts"], 12)
            chain(dve.tensor_scalar(row_lo[:, :], row[:, :], G - 1, None, ALU.bitwise_and))
            chained()
            chain(dve.tensor_scalar(row_exp[:, :], row_lo[:, :], 127 + 9, None, ALU.add))
            chained()
            chain(dve.tensor_scalar(row_pow[:, :], row_exp[:, :], 23, None, ALU.logical_shift_left))
            chained()
            dve.tensor_scalar(pack[:, :], group[:, :], row_pow[:, :].bitcast(F32), None, ALU.mult).then_inc(s["dc"], 1)

            def keys(c):
                words = PS[:, c, :].rearrange("p (t w) -> p t w", w=WC)
                k = key[:, c % 2, :, :]
                dve.wait_ge(s["packed"], c + 1)
                chain(dve.scalar_tensor_tensor(out=k, in0=words, scalar=0.0,
                                               in1=iota_w[:, None, c * WC:c * WC + WC].to_broadcast([P, T, WC]),
                                               op0=ALU.is_gt, op1=ALU.mult))
                chained()
                chain(dve.scalar_tensor_tensor(out=k, in0=k, scalar=65536.0, in1=words, op0=ALU.mult, op1=ALU.add))
                chained()

            def tops(c, level):
                if 0 < c < C:
                    for t in range(T * level // 8, T * (level + 1) // 8):
                        chain(dve.max(top_words[:, c, t, :], key[:, c % 2, t, :]))

            def list_part(c):
                n = chain(dve.tensor_copy(top_u[:, :, :], top_words[:, c, :, :]))
                tops(c + 1, 0)
                chained(n)
                chain(dve.tensor_scalar(word_u[:, :, :], top_u[:, :, :], 16, None, ALU.logical_shift_right))
                n = chain(dve.tensor_scalar(bits_u[:, :, :], top_u[:, :, :], 0xFFFF, None, ALU.bitwise_and))
                tops(c + 1, 1)
                chained(n)
                chain(dve.tensor_scalar(base[:, :, :], word_u[:, :, :], float(G), 1.0 - 127.0, ALU.mult, ALU.add))
                n = chain(dve.tensor_copy(bits_f[:, :, :], bits_u[:, :, :]))
                tops(c + 1, 2)
                chained(n)
                chain(dve.tensor_scalar(first_e[:, :, :], bits_f[:, :, :].bitcast(U32), 23, None, ALU.logical_shift_right))
                n = chain(dve.tensor_scalar(first_p[:, :, :].bitcast(U32), bits_f[:, :, :].bitcast(U32), 0x7F800000, None,
                                            ALU.bitwise_and))
                tops(c + 1, 3)
                chained(n)
                chain(dve.tensor_tensor(rest[:, :, :], bits_f[:, :, :], first_p[:, :, :], ALU.subtract))
                n = chain(dve.tensor_tensor(code1[:, :, :], first_e[:, :, :], base[:, :, :], ALU.add))
                tops(c + 1, 4)
                chained(n)
                chain(dve.tensor_scalar(second_e[:, :, :], rest[:, :, :].bitcast(U32), 23, None, ALU.logical_shift_right))
                chain(dve.tensor_scalar(second_p[:, :, :].bitcast(U32), rest[:, :, :].bitcast(U32), 0x7F800000, None,
                                        ALU.bitwise_and))
                n = chain(dve.scalar_tensor_tensor(out=codes[:, :, c, 0, :], in0=bits_f[:, :, :], scalar=0.0,
                                                   in1=code1[:, :, :], op0=ALU.is_gt, op1=ALU.mult))
                tops(c + 1, 5)
                chained(n)
                chain(dve.tensor_tensor(rest2[:, c, :, :], rest[:, :, :], second_p[:, :, :], ALU.subtract))
                n = chain(dve.tensor_tensor(code2[:, :, :], second_e[:, :, :], base[:, :, :], ALU.add))
                tops(c + 1, 6)
                tops(c + 1, 7)
                chained(n)
                chain(dve.scalar_tensor_tensor(out=codes[:, :, c, 1, :], in0=rest[:, :, :], scalar=0.0,
                                               in1=code2[:, :, :], op0=ALU.is_gt, op1=ALU.mult))
                chained()

            for c in range(C):
                if c == 0:
                    keys(c)
                    for t in range(T):
                        chain(dve.max(top_words[:, c, t, :], key[:, c % 2, t, :]))
                    chained()
                if c < C - 1:
                    keys(c + 1)
                list_part(c)
            chained()
            all_codes = codes[:, :, :, :, :].rearrange("p t c s k -> p t (c s k)")
            for t in range(T):
                chain(dve.max(nbr[:, t, 0:8], all_codes[:, t, :]))
            chained()
            for t in range(T):
                chain(dve.match_replace(out=all_codes[:, t, :], in_to_replace=nbr[:, t, 0:8],
                                        in_values=all_codes[:, t, :], imm_value=0.0))
            chained()
            for t in range(T):
                chain(dve.max(nbr[:, t, 8:16], all_codes[:, t, :]))
            chained()
            chain(dve.tensor_scalar(picked[:, :, 0, :], nbr[:, :, :], 0.0, None, ALU.is_gt))
            chained()
            dve.reduce_sum(deg[:, :], picked[:, :, 0, :], axis=AX).then_inc(s["nbrs"], 1)
            chain(dve.tensor_copy(per_query[:, :, 0:K], nbr[:, :, :]))
            chain(dve.tensor_copy(per_query[:, :, K], row_f[:, :].to_broadcast([P, T])))
            dve.wait_ge(s["nbrs"], 1)
            chain(dve.tensor_scalar(half[:, :], deg[:, :], 0.5, None, ALU.mult))
            chain(dve.tensor_scalar(start_half[:, :], deg[:, :], -0.5, 0.5, ALU.mult, ALU.add))
            dve.wait_ge(s["off_ps"], 1)
            chained()
            dve.tensor_tensor(shift[:, :], start_half[:, :], PS[:, 0, 0:T], ALU.subtract).then_inc(s["shifts"], 1)
            chain(dve.tensor_copy(per_query[:, :, K + 1], PS[:, 0, 0:T]))
            chained()
            dve.reduce_max(count[:, :], PS[:, 0, T:2 * T], axis=AX).then_inc(s["off_read"], 1)

            QT = T // LISTS

            def what_edges_get(i):
                tiles = slice(i * QT, i * QT + QT)
                dve.wait_ge(s["l_ps"], i + 1)
                chain(dve.tensor_copy(L[:, tiles, :, :],
                                      PS[:, 4 + i % 2, 0:QT * LP].rearrange("p (t l) -> p t l", l=LP)[:, :, 0:U * LR]
                                      .rearrange("p t (u l) -> p t u l", u=U)))
                chained()
                chain(dve.tensor_tensor(k_of[:, tiles, :], iota_e[:, None, :].to_broadcast([P, QT, U]),
                                        L[:, tiles, :, K + 1], ALU.subtract))
                chained()
                chain(dve.tensor_tensor(k_hot[:, tiles, :, :].rearrange("p t u k -> p (t u) k"),
                                        iota_k[:, None, :].to_broadcast([P, QT * U, K]),
                                        k_of[:, tiles, :].rearrange("p t u -> p (t u)")[:, :, None]
                                        .to_broadcast([P, QT * U, K]), ALU.is_equal))
                chained()
                chain(dve.tensor_tensor(picked[:, tiles, :, :], k_hot[:, tiles, :, :], L[:, tiles, :, 0:K], ALU.mult))
                chained()
                chain(dve.reduce_sum(code_e[:, tiles, :], picked[:, tiles, :, :], axis=AX))
                chained()
                dve.tensor_scalar(key_row[:, tiles, :], code_e[:, tiles, :], 1.0, 0.0, ALU.subtract,
                                  ALU.max).then_inc(s["listed"], 1)

            for step in range(T + 2):
                if step < T:
                    dve.wait_ge(s["dist_ready"], step + 1)
                    dve.tensor_scalar(own[:, step, :], dist[:, step % 4, :], half[:, step:step + 1], None,
                                      ALU.is_lt).then_inc(s["own_ready"], 1)
                t = step - 2
                if t >= 0 and t % 2 == 1:
                    dve.wait_ge(s["own_t_ps"], t + 1)
                    dve.tensor_copy(own_t[:, t, :, :], PS[:, t % 4, 0:E // 2].bitcast(F16)
                                    .rearrange("p (u n) -> p u n", u=U)).then_inc(s["own_t_dve"], 1)
                if t % QT == QT - 1 and t > 0:
                    what_edges_get(t // QT)
            chain(dve.tensor_scalar(no_slot[:, :, :], nbr[:, :, :], 0.0, NO_EDGE, ALU.is_equal, ALU.mult))
            def capacity():
                dve.wait_ge(s["off_read"], 1)
                chain(dve.tensor_scalar(over[:, 0:1], count[:, :], float(E), None, ALU.subtract))
                chain(dve.reduce_max(over[:, 1:2], rest2[:, :, :, :].rearrange("p c t k -> p (c t k)"), axis=AX))
                chain(dve.reduce_max(over[:, 2:3], top_words[:, :, :, KC - 1].rearrange("p c t -> p (c t)"), axis=AX))
                chain(dve.reduce_max(over[:, 3:4], nbr[:, :, K - 1], axis=AX))
                chained()
                chain(dve.reduce_max(over1[:, :], over[:, :], axis=AX))
                chained()
                dve.tensor_scalar(over2[:, :], over1[:, :], 0.0, None, ALU.is_gt).then_inc(s["over_ready"], 1)

            def product_of(layer, p, i):
                if not among(p):
                    return
                t, n = 2 * p + i // U, i % U
                if n == 0:
                    need(dve, "ds_ready", layer * PAIRS + p - 1)
                    dve.wait_ge(s["qe_ready"], layer * T + t + 1)
                    dve.wait_ge(gathered[t % RING], ((layer * T + t) // RING + 1) * 16 * U)
                dve.tensor_tensor_reduce(
                    out=prod[:, i // U, n, :], in0=expanded(i // U, n), in1=xg[:, t % RING, n, :], op0=ALU.mult,
                    op1=ALU.add, scale=-1.0, scalar=0.0, accum_out=neg_score[:, p % 2, i:i + 1]).then_inc(s["s_done"], 1)

            def top_of_edges(layer, k):
                if not among(k):
                    return
                dve.wait_ge(s["me_ready"], layer * PAIRS + k + 1)
                need(dve, "ds_ready", layer * PAIRS + k)
                chains["top"] = chain(dve.reduce_sum(edge_top[:, :], PS[:, 6, 0:2 * U * S3].rearrange("p (u s) -> p u s", s=S3),
                                                     axis=AX))

            def less_top(layer, k):
                if not among(k):
                    return
                chained(chains["top"])
                need(dve, "p_ready", layer * PAIRS + k)
                dve.tensor_tensor(shifted[:, :], neg_score[:, k % 2, :], edge_top[:, :],
                                  ALU.subtract).then_inc(s["ds_ready"], 1)

            def norm_level(layer, k, level):
                if not among(k):
                    return
                if level > 0:
                    chained(chains["norm"])
                if level == 0:
                    dve.wait_ge(s["stats"], (layer * PAIRS + k + 1) * 2)
                    need(dve, "normed", layer * T + 2 * k)
                    for j in range(2):
                        n = chain(dve.bn_aggr(moment[:, j, :], bn_pair[:, j, :]))
                elif level == 1:
                    chain(dve.tensor_scalar(less_half[:, :], moment[:, :, 1], EPS, -0.5, ALU.add, ALU.mult))
                    n = chain(dve.tensor_scalar(var_pair[:, :], moment[:, :, 1], EPS, None, ALU.add))
                elif level == 2:
                    n = chain(dve.tensor_scalar(guess[:, :].bitcast(U32), var_pair[:, :].bitcast(U32), -0.5,
                                                float(0x5F3759DF), ALU.mult, ALU.add))
                elif level in (3, 5, 7):
                    for j in range(2):
                        n = chain(dve.tensor_scalar(near[:, j:j + 1], guess[:, j:j + 1], guess[:, j:j + 1],
                                                    less_half[:, j:j + 1], ALU.mult, ALU.mult))
                elif level in (4, 6, 8):
                    n = chain(dve.scalar_tensor_tensor(out=guess[:, :], in0=near[:, :], scalar=1.5, in1=guess[:, :],
                                                       op0=ALU.add, op1=ALU.mult))
                else:
                    for j in range(2):
                        xn = X[layer + 1][:, 2 * k + j, :]
                        dve.tensor_scalar(xn, xn, moment[:, j, 0:1], guess[:, j:j + 1], ALU.subtract,
                                          ALU.mult).then_inc(s["normed"], 1)
                    return
                chains["norm"] = n

            def residual(layer, k, j):
                if not among(k):
                    return
                t = 2 * k + j
                dve.wait_ge(s["o_ready"], layer * PAIRS + k + 1)
                dve.scalar_tensor_tensor(out=X[layer + 1][:, t, :], in0=PS[:, 6, j * D:j * D + D], scalar=inv[:, t:t + 1],
                                         in1=X[layer][:, t, :], op0=ALU.mult, op1=ALU.add).then_inc(s["res"], 1)

            def row_stats(layer, k, j):
                if not among(k):
                    return
                dve.wait_ge(s["res"], layer * T + 2 * k + j + 2)
                dve.bn_stats(bn_pair[:, j, :], X[layer + 1][:, 2 * k + j, :]).then_inc(s["stats"], 1)

            for layer in range(LAYERS):
                if layer == LAYERS - 1:
                    dve.wait_ge(s["flag_ps"], 1)
                    dve.tensor_copy(over_i[:, :], PS[:, 0, 0:1]).then_inc(s["flag"], 1)
                for p in range(PAIRS + 3):
                    now = layer * PAIRS + p
                    k = p - 3
                    for i in range(2 * U):
                        product_of(layer, p, i)
                        norm_level(layer, k, i)
                        if i == SHIFT_AT - 1:
                            top_of_edges(layer, p - 1)
                        if i == SHIFT_AT:
                            less_top(layer, p - 1)
                    if among(p):
                        dve.wait_ge(s["s_done"], (now + 1) * 2 * U)
                        first = chain(dve.tensor_copy(s_part[:, :, 0], neg_score[:, p % 2, :]))
                        norm_level(layer, k, 6)
                        chained(first)
                        chain(dve.tensor_tensor(s_part[:, :, 1], neg_score[:, p % 2, :], s_part[:, :, 0], ALU.subtract))
                        second = chain(dve.tensor_tensor(s_rest[:, :], neg_score[:, p % 2, :], s_part[:, :, 0], ALU.subtract))
                        norm_level(layer, k, 7)
                        chained(second)
                        third = chain(dve.tensor_tensor(s_part[:, :, 2], s_rest[:, :], s_part[:, :, 1], ALU.subtract))
                        norm_level(layer, k, 8)
                        chained(third)
                        dve.tensor_tensor(score_k[:, :, :, :],
                                          k_hot[:, 2 * p:2 * p + 2, :, :].rearrange("p t u k -> p (t u) k")[:, :, None, :]
                                          .to_broadcast([P, 2 * U, S3, K]),
                                          s_part[:, :, :, None].to_broadcast([P, 2 * U, S3, K]),
                                          ALU.mult).then_inc(s["sk_in"], 1)
                    else:
                        for level in (6, 7, 8):
                            norm_level(layer, k, level)
                    if layer == 0 and p == PAIRS + 1:
                        capacity()
                    residual(layer, p - 2, 0)
                    norm_level(layer, k, 9)
                    residual(layer, p - 2, 1)
                    if among(p):
                        dve.wait_ge(s["sk_ready"], now + 1)
                        need(dve, "totalled", 2 * now)
                        dve.tensor_reduce(out=neg_top[:, :], in_=PS[:, 4, 0:2 * K].rearrange("p (j k) -> p j k", j=2),
                                          axis=AX, op=ALU.min).then_inc(s["topped"], 1)
                        row_stats(layer, p - 2, 0)
                        dve.wait_ge(s["topped"], now + 1)
                        n = chain(dve.tensor_copy(top_part[:, :, 0], neg_top[:, :]))
                        row_stats(layer, p - 2, 1)
                        chained(n)
                        chain(dve.tensor_tensor(top_part[:, :, 1], neg_top[:, :], top_part[:, :, 0], ALU.subtract))
                        chain(dve.tensor_tensor(top_rest[:, :], neg_top[:, :], top_part[:, :, 0], ALU.subtract))
                        chained()
                        dve.tensor_tensor(top_part[:, :, 2], top_rest[:, :], top_part[:, :, 1],
                                          ALU.subtract).then_inc(s["top_split"], 1)
                        dve.wait_ge(s["totalled"], 2 * (now + 1))
                        need(dve, "res", layer * T + 1)
                        chain(dve.reciprocal(inv[:, 2 * p:2 * p + 2], total[:, 2 * p:2 * p + 2]))
                    else:
                        row_stats(layer, p - 2, 0)
                        row_stats(layer, p - 2, 1)
                    if among(p - 1):
                        chained()

            with too_many(dve):
                for c, n in enumerate(("xt_ps", "xt_sb", "res", "kept")):
                    dve.memset(started[:, 2 + c:3 + c], 0.0).then_inc(sa[n], 1)
                for layer in range(LAYERS):
                    with dve.Fori(0, T) as t:
                        dve.tensor_scalar(not_adj[:, :, :], adj_words[:, :, bass.ds(t * (P // 4), P // 4)], 0x01010101,
                                          None, ALU.bitwise_xor).then_inc(sa["slab"], 1)
                        dve.wait_ge(sa["scored"], t + (layer * T + 1))
                        dve.reduce_max(row_top[:, :], PS[:, 0:4, :].rearrange("p b n -> p (b n)"),
                                       axis=AX).then_inc(sa["topped"], 1)
                        dve.wait_ge(sa["topped"], t + (layer * T + 1))
                        dve.tensor_scalar(row_neg_top[:, :], row_top[:, :], -1.0, None, ALU.mult).then_inc(sa["neg_topped"], 1)
                        dve.tensor_scalar(row_has[:, :], row_top[:, :], NO_EDGE / 2, None, ALU.is_gt).then_inc(sa["has"], 1)
                        dve.wait_ge(sa["exped"], t + (layer * T + 1))
                        dve.reciprocal(row_inv[:, :], row_total[:, :]).then_inc(sa["inved"], 1)
                        dve.wait_ge(sa["inved"], t + (layer * T + 1))
                        dve.tensor_tensor(row_scale[:, :], row_inv[:, :], row_has[:, :], ALU.mult).then_inc(sa["scaled"], 1)
                        for c in (0, 2):
                            dve.wait_ge(sa["t_ps"], t * 4 + (layer * T * 4 + c + 1))
                            dve.tensor_copy(all_probT[:, 4 * c:4 * c + 4, :],
                                            PS[:, 4, :].rearrange("p (k n) -> p k n", k=4)).then_inc(sa["t_dve"], 1)
                        dve.wait_ge(sa["o_ps"], t + (layer * T + 1))
                        dve.wait_ge(sa["kept"], t + (layer * T + 1))
                        dve.scalar_tensor_tensor(out=new_row[:, :], in0=PS[:, 6, D:2 * D], scalar=row_scale[:, :],
                                                 in1=tile(X[layer], t), op0=ALU.mult, op1=ALU.add).then_inc(sa["res"], 1)
                        dve.wait_ge(sa["res"], t + (layer * T + 2))
                        dve.bn_stats(bn_row[:, :], new_row[:, :]).then_inc(sa["stat"], 1)
                        dve.wait_ge(sa["stat"], t + (layer * T + 1))
                        dve.tensor_copy(tile(bn, t), bn_row[:, :]).then_inc(sa["moved"], 1)
                    dve.wait_ge(sa["moved"], T * (layer + 1))
                    moments(sa, layer)
                    dve.wait_ge(sa["kept"], T * (layer + 1) + 1)
                    with dve.Fori(0, T) as t:
                        xn = tile(X[layer + 1], t)
                        dve.tensor_scalar(xn, xn, mean[:, bass.ds(t, 1)], rstd[:, bass.ds(t, 1)],
                                          ALU.subtract, ALU.mult).then_inc(sa["normed"], 1)

        @block.tensor
        def _(pe):
            def product(n):
                for h in range(H):
                    for e in range(H):
                        last = nc.tensor.matmul(PS[:, 6, h * D:h * D + D], W[:, n, 0, e, h * P:h * P + P], W[:, n, 1, e, :],
                                                start=(e == 0), stop=(e == H - 1))
                last.then_inc(s["m_ps"], 1)

            def turned(n, bank):
                for h in range(H):
                    for e in range(H):
                        last = nc.tensor.transpose(PS[:, bank, h * D + e * P:h * D + e * P + P],
                                                   W[:, n, 2, e, h * P:h * P + P], ident[:, :])
                last.then_inc(s["m_ps"], 1)

            def pack_part(c):
                pe.wait_ge(a_in[c], 16)
                for j in range(4 * c, 4 * c + 4):
                    for t in range(T):
                        at_w = t * WC + (j % 4) * WT
                        last = nc.tensor.matmul(PS[:, c, at_w:at_w + WT],
                                                adj_words[:, j, t * (P // 4):(t + 1) * (P // 4)].bitcast(FP8), pack[:, :],
                                                start=True, stop=True)
                last.then_inc(s["packed"], 1)

            pe.wait_ge(s["consts"], 12)
            pe.wait_ge(s["dc"], 1)
            pack_part(0)
            pack_part(1)
            pe.wait_ge(s["w_first"], 32)
            product(0)
            pe.wait_ge(s["x_in"], 16)
            def transposes(rows, k, bank):
                for j in range(2):
                    for h in range(H):
                        at_h = j * D + h * P
                        last = nc.tensor.transpose(PS[:, bank, at_h:at_h + P], rows[:, 2 * k + j, h * P:h * P + P],
                                                   ident[:, :])
                last.then_inc(s["xt_ps"], 1)

            def queries(layer, turned_rows, bank):
                for j in range(2):
                    for h in range(H):
                        last = nc.tensor.matmul(PS[:, bank, j * D:j * D + D], turned_rows[:, j, h, :], M[:, layer, h, :],
                                                start=(j == 0 and h == 0), stop=(h == H - 1), skip_group_check=True)
                last.then_inc(s["q_ps"], 1)

            def less(k, part, bank, read, done, nth):
                pe.wait_ge(s[read], nth)
                for j in range(2):
                    last = nc.tensor.matmul(PS[:, bank, j * D:j * D + D], minus[:, :], Q[:, 2 * k + j, part, :],
                                            start=False, stop=True, skip_group_check=True)
                last.then_inc(s[done], 1)

            def offsets():
                pe.wait_ge(s["nbrs"], 1)
                nc.tensor.matmul(PS[:, 0, 0:T], before[:, :], deg[:, :], start=True, stop=True)
                nc.tensor.matmul(PS[:, 0, T:2 * T], ones[:, :], deg[:, :], start=True, stop=True).then_inc(s["off_ps"], 1)

            for i in range(FIRST + 3):
                if 2 * i == T // 2:
                    pe.wait_ge(s["x_rest_in"], 16)
                if i < FIRST:
                    need(pe, "xt_sb", i)
                    transposes(X0, i, 4)
                if i == 1:
                    pe.wait_ge(s["m_sb"], 1)
                if 0 <= i - 1 < FIRST:
                    pe.wait_ge(s["xt_sb"], i)
                    need(pe, "q_lo", i - 3)
                    queries(0, first_xt[(i - 1) % 2], 5 + (i - 1) % 3)
                if 0 <= i - 2 < FIRST:
                    less(i - 2, 0, 5 + (i - 2) % 3, "q_hi", "q_less_hi", i - 1)
                if 0 <= i - 3 < FIRST:
                    less(i - 3, 1, 5 + (i - 3) % 3, "q_mid", "q_less_mid", i - 2)
                if i in PACK_AT:
                    pack_part(2 + PACK_AT.index(i))
                if i == OFFSETS_AT:
                    offsets()
            QT = T // LISTS
            pe.wait_ge(s["off_read"], 1)
            for t in range(T):
                pe.wait_ge(s["own_ready"], t + 1)
                if t % QT == 0 and t >= 2 * QT:
                    pe.wait_ge(s["listed"], t // QT - 1)
                for n in range(U):
                    at_l = t % QT * LP + n * LR
                    last = nc.tensor.matmul(PS[:, 4 + t // QT % 2, at_l:at_l + LR], own[:, t, n * P:n * P + P],
                                            per_query[:, t, :], start=True, stop=True)
                if t % QT == QT - 1:
                    last.then_inc(s["l_ps"], 1)
                if t >= 4:
                    pe.wait_ge(s["own_t_dve" if t % 2 else "own_t_act"], t // 2 - 1)
                for n in range(U):
                    last = nc.tensor.transpose(PS[:, t % 4, n * (P // 2):n * (P // 2) + P // 2].bitcast(F16),
                                               own[:, t, n * P:n * P + P], ident_h[:, :])
                last.then_inc(s["own_t_ps"], 1)
                if t == T // 2:
                    pe.wait_ge(s["q_lo"], FIRST)
                    pe.wait_ge(s["w_in"], 64)
                    turned(0, 7)
                    product(1)
            pe.wait_ge(s["own_t_act"], T // 2)
            pe.wait_ge(s["own_t_dve"], T // 2)

            def expand(layer, t):
                pe.wait_ge(s["q_lo"], layer * PAIRS + t // 2 + 1)
                need(pe, "s_done", (layer * T + t - 1) * U)
                for n in range(U):
                    for part in range(S3):
                        last = nc.tensor.matmul(expanded(t % 2, n), own[:, t, n * P:n * P + P], Q[:, t, part, :],
                                                start=(part == 0), stop=(part == S3 - 1))
                last.then_inc(s["qe_ready"], 1)

            def sums(layer, t):
                pe.wait_ge(s["a_ready"], (layer * T + t + 1) * U)
                need(pe, "y_sb_ready", layer * PAIRS + t // 2)
                pe.wait_ge(s["m_sb"], 4)
                for h in range(H):
                    at_h = t % 2 * D + h * P
                    for n in range(U):
                        last = nc.tensor.matmul(PS[:, 5, at_h:at_h + P], xg[:, t % RING, n, h * P:h * P + P],
                                                weight[:, t % 2, n, :], start=(n == 0), stop=(n == U - 1))
                last.then_inc(s["y_ready"], 1)

            def projected(layer, k):
                pe.wait_ge(s["y_sb_ready"], layer * PAIRS + k + 1)
                pe.wait_ge(s["ds_ready"], layer * PAIRS + min(k + 2, PAIRS))
                need(pe, "res", layer * T + 2 * k + 1)
                for j in range(2):
                    for h in range(H):
                        last = nc.tensor.matmul(PS[:, 6, j * D:j * D + D], y_sb[:, j, h, :], WvT[:, layer, h, :],
                                                start=(h == 0), stop=(h == H - 1))
                last.then_inc(s["o_ready"], 1)

            for layer in range(LAYERS):
                if layer == LAYERS - 1:
                    pe.wait_ge(s["over_ready"], 1)
                    pe.wait_ge(s["s_done"], layer * T * U)
                    nc.tensor.matmul(PS[:, 0, 0:1], ones[:, :], over2[:, :], start=True, stop=True).then_inc(s["flag_ps"], 1)
                    pe.wait_ge(s["flag"], 1)
                for p in range(STEPS):
                    now = layer * PAIRS + p
                    if p == 0:
                        expand(layer, 0)
                    if among(p):
                        expand(layer, 2 * p + 1)
                    if p == PAIRS:
                        projected(layer, p - 2)
                    if p == PAIRS:
                        sums(layer, 2 * p - 2)
                        sums(layer, 2 * p - 1)
                    if (z := asked(layer, p)) is not None:
                        pe.wait_ge(s["xt_sb"], z + 1)
                        queries(z // PAIRS, xt, 7)
                    if 2 <= p < PAIRS:
                        projected(layer, p - 2)
                    if p == PAIRS:
                        projected(layer, p - 1)
                    if z is not None:
                        less(z % PAIRS, 0, 7, "q_hi", "q_less_hi", z + 1)
                    if 0 < p < PAIRS:
                        sums(layer, 2 * p - 2)
                    if z is not None:
                        less(z % PAIRS, 1, 7, "q_mid", "q_less_mid", z + 1)
                    if among(p):
                        pe.wait_ge(s["sk_in"], now + 1)
                        need(pe, "totalled", 2 * now)
                        for j in range(2):
                            scores = PS[:, 4, j * K:(j + 1) * K]
                            nc.tensor.matmul(scores, minus[:, :], no_slot[:, 2 * p + j, :], start=True, stop=False)
                            for n in range(U):
                                for part in range(S3):
                                    last = nc.tensor.matmul(scores, own_t[:, 2 * p + j, n, :],
                                                            score_k[:, j * U + n, part, :], start=False,
                                                            stop=(n == U - 1 and part == S3 - 1))
                        last.then_inc(s["sk_ready"], 1)
                    if layer == 0 and p == 0:
                        turned(1, 5)
                        pe.wait_ge(s["m_sb"], 3)
                    if among(p + 1):
                        expand(layer, 2 * p + 2)
                    if 0 < p < PAIRS:
                        sums(layer, 2 * p - 1)
                    if among(p):
                        pe.wait_ge(s["top_split"], now + 1)
                        for j in range(2):
                            for n in range(U):
                                at_m = (j * U + n) * S3
                                last = nc.tensor.matmul(PS[:, 6, at_m:at_m + S3], own[:, 2 * p + j, n * P:n * P + P],
                                                        top_part[:, j, :], start=True, stop=True)
                        last.then_inc(s["me_ready"], 1)
                    if (z := turned_for(layer, p)) is not None:
                        if z >= PAIRS:
                            pe.wait_ge(s["normed"], 2 * (z - PAIRS) + 2)
                        pe.wait_ge(s["q_lo"], z)
                        transposes(X[z // PAIRS], z % PAIRS, 7)

            with too_many(pe):
                pe.wait_ge(sa["no_edge"], 1)
                for layer in range(LAYERS):
                    with pe.Fori(0, T) as t:
                        pe.wait_ge(sa["staged"], t + (layer * T + 1))
                        pe.wait_ge(sa["xt_sb"], t + (layer * T + 1))
                        for h in range(H):
                            last = nc.tensor.transpose(PS[:, 6, h * P:h * P + P], one_row[:, h * P:h * P + P], ident[:, :])
                        last.then_inc(sa["xt_ps"], 1)
                    pe.wait_ge(sa["xt_sb"], T * (layer + 1) + 1)
                    with pe.Fori(0, T) as t:
                        pe.wait_ge(sa["res"], t + (layer * T + 1))
                        pe.wait_ge(sa["slab"], t + (layer * T + 1))
                        for h in range(H):
                            for e in range(H):
                                last = nc.tensor.matmul(PS[:, 6, h * P:h * P + P], M[:, layer, e, h * P:h * P + P],
                                                        all_xT[:, e, bass.ds(t * P, P)], start=(e == 0), stop=(e == H - 1))
                        last.then_inc(sa["q_ps"], 1)
                        for j in range(T):
                            nc.tensor.matmul(PS[:, j // 4, (j % 4) * P:(j % 4) * P + P], not_adj[:, j, :].bitcast(FP8),
                                             no_edge_ident[:, :], start=(j % 4 == 0), stop=False, skip_group_check=True)
                        pe.wait_ge(sa["q_sb"], t + (layer * T + 1))
                        for h in range(H):
                            for c in range(4):
                                last = nc.tensor.matmul(PS[:, c, :], one_qT[:, h, :], all_xT[:, h, c * BANK:c * BANK + BANK],
                                                        start=False, stop=(h == H - 1), skip_group_check=True)
                        last.then_inc(sa["scored"], 1)
                        pe.wait_ge(sa["exped"], t + (layer * T + 1))
                        for c in range(4):
                            if c == 2:
                                pe.wait_ge(sa["t_dve"], t * 2 + (layer * T * 2 + 1))
                            if c == 3:
                                pe.wait_ge(sa["t_act"], t * 2 + (layer * T * 2 + 1))
                            for k in range(4):
                                j = 4 * c + k
                                last = nc.tensor.transpose(PS[:, 4 + c % 2, k * P:k * P + P], all_prob[:, j * P:j * P + P],
                                                           ident[:, :])
                            last.then_inc(sa["t_ps"], 1)
                        pe.wait_ge(sa["t_dve"], t * 2 + (layer * T * 2 + 2))
                        pe.wait_ge(sa["t_act"], t * 2 + (layer * T * 2 + 2))
                        for h in range(H):
                            for j in range(T):
                                last = nc.tensor.matmul(PS[:, 7, h * P:h * P + P], X[layer][:, j, h * P:h * P + P],
                                                        all_probT[:, j, :], start=(j == 0), stop=(j == T - 1))
                        last.then_inc(sa["y_ps"], 1)
                        pe.wait_ge(sa["y_sb"], t + (layer * T + 1))
                        for h in range(H):
                            last = nc.tensor.matmul(PS[:, 6, D:2 * D], y_sb[:, 0, h, :], WvT[:, layer, h, :],
                                                    start=(h == 0), stop=(h == H - 1))
                        last.then_inc(sa["o_ps"], 1)


def kernel(**inputs):
    import numpy as np
    import concourse.bacc as bacc
    from concourse.bass_utils import run_bass_kernel_spmd as run

    nc = bacc.Bacc("TRN2", target_bir_lowering=False, num_devices=1)
    arrays, ap = {}, {}
    for name, value in inputs.items():
        a = np.ascontiguousarray(value)
        if a.dtype == np.bool_:
            a = a.view(np.uint32)
        arrays[f"in_{name}"] = a
        ap[name] = nc.dram_tensor(f"in_{name}", a.shape, mybir.dt.from_np(a.dtype), kind="ExternalInput").ap()
    out = nc.dram_tensor("out", (N, D), F32, kind="ExternalOutput").ap()
    w = {k: [ap[f"L{n}_gnn_W{k}"] for n in range(LAYERS)] for k in "qkv"}
    edges_and_dense(nc, ap["x"], ap["adj"], w["q"], w["k"], w["v"], out)
    return run(nc, [arrays], core_ids=[0]).results[0]["out"]
```
